# Optimizing a Trainium2 kernel written in Bass

```python
import numpy as np
import jax
import jax.numpy as jnp

def _softmax(x, axis=-1):
    return jax.nn.softmax(x, axis=axis)

def _gelu(x):
    return jax.nn.gelu(x, approximate=True)

def _silu(x):
    return jax.nn.silu(x)

def _sigmoid(x):
    return jax.nn.sigmoid(x)

def _layernorm(x, axis=-1, eps=1e-05):
    m = jnp.mean(x, axis=axis, keepdims=True)
    v = jnp.var(x, axis=axis, keepdims=True)
    return (x - m) / jnp.sqrt(v + eps)

def _scatter_add(tgt, idx, src, axis=0):
    return tgt.at[idx].add(src)

def _segment_sum(src, seg, n):
    return jax.ops.segment_sum(src, seg, n)
kernel_name = 'mk_macaron_d1_jaxref_r4_6a38c8'

def setup_inputs(seed: int=0):
    np.random.seed(seed)
    _w = jnp.asarray

    def _L0_attn_setup():
        import math
        import jax, jax.numpy as jnp
        import numpy as np
        D_MODEL = 1024
        N_HEADS = 32
        N_KV_HEADS = 8
        D_HEAD = D_MODEL // N_HEADS
        GROUP = N_HEADS // N_KV_HEADS
        ROPE = dict(rope_theta=500000.0, factor=32.0, hi_freq_factor=4.0, lo_freq_factor=1.0, original_context_length=2048)

        def _rope_cos_sin(head_dim, pos, dtype):
            idx = jnp.arange(0, head_dim, 2, dtype=jnp.float32) / head_dim
            freq = 1.0 / (2.0 * math.pi) * ROPE['rope_theta'] ** (-idx)
            factor, lo, hi = (ROPE['factor'], ROPE['lo_freq_factor'], ROPE['hi_freq_factor'])
            L0 = ROPE['original_context_length']
            freq_low, freq_high = (lo / L0, hi / L0)
            freq_scaled = jnp.where(freq < freq_low, freq / factor, freq)
            smooth = jnp.clip((L0 * freq - lo) / (hi - lo), 0.0, 1.0)
            freq_smooth = (1.0 - smooth) * (freq / factor) + smooth * freq
            is_mid = (freq >= freq_low) & (freq <= freq_high)
            freq = jnp.where(is_mid, freq_smooth, freq_scaled)
            phase = 2.0 * math.pi * pos.astype(jnp.float32)[:, None] * freq[None, :]
            emb = jnp.concatenate([phase, phase], axis=-1)
            return (jnp.cos(emb).astype(dtype), jnp.sin(emb).astype(dtype))

        def _rotate_half(x):
            h = x.shape[-1] // 2
            return jnp.concatenate([-x[..., h:], x[..., :h]], axis=-1)
        key = jax.random.key(seed)
        ks = jax.random.split(key, 5)
        B, T = (1, 512)
        s = 0.02
        return {'resid': jax.random.normal(ks[0], (B, T, D_MODEL), jnp.float32), 'Wq': jax.random.normal(ks[1], (D_MODEL, D_MODEL), jnp.float32) * s, 'Wk': jax.random.normal(ks[2], (D_MODEL, N_KV_HEADS * D_HEAD), jnp.float32) * s, 'Wv': jax.random.normal(ks[3], (D_MODEL, N_KV_HEADS * D_HEAD), jnp.float32) * s, 'Wo': jax.random.normal(ks[4], (D_MODEL, D_MODEL), jnp.float32) * s}
    _L0_attn_in = _L0_attn_setup()

    def _L0_ffn_setup():
        import jax, jax.numpy as jnp
        import numpy as np
        B, S, D_IN, D_OUT = (2, 512, 1024, 1024)
        E, K, R = (8, 2, 16)
        SCALING = 32.0 / 16.0
        key = jax.random.key(seed)
        ks = jax.random.split(key, 6)
        x = jax.random.normal(ks[0], (B, S, D_IN), dtype=jnp.float32)
        gate_w = jax.random.normal(ks[1], (E, D_IN), dtype=jnp.float32) * 0.02
        base_w = jax.random.normal(ks[2], (D_OUT, D_IN), dtype=jnp.float32) * 0.02
        base_b = jax.random.normal(ks[3], (D_OUT,), dtype=jnp.float32) * 0.02
        lora_A = jax.random.normal(ks[4], (E, R, D_IN), dtype=jnp.float32) * 0.02
        lora_B = jax.random.normal(ks[5], (E, D_OUT, R), dtype=jnp.float32) * 0.02
        return {'x': x, 'gate_w': gate_w, 'base_w': base_w, 'base_b': base_b, 'lora_A': lora_A, 'lora_B': lora_B}
    _L0_ffn_in = _L0_ffn_setup()
    _d = {'L0_attn_resid': _L0_attn_in['resid'], 'L0_attn_Wq': _L0_attn_in['Wq'], 'L0_attn_Wk': _L0_attn_in['Wk'], 'L0_attn_Wv': _L0_attn_in['Wv'], 'L0_attn_Wo': _L0_attn_in['Wo'], 'L0_ffn_gate_w': _L0_ffn_in['gate_w'], 'L0_ffn_base_w': _L0_ffn_in['base_w'], 'L0_ffn_base_b': _L0_ffn_in['base_b'], 'L0_ffn_lora_A': _L0_ffn_in['lora_A'], 'L0_ffn_lora_B': _L0_ffn_in['lora_B']}
    _x0 = _d['L0_attn_resid']
    _d['L0_attn_resid'] = jax.random.normal(jax.random.fold_in(jax.random.key(seed), 1), (2, 1024, 1024), dtype=_x0.dtype)
    del _x0
    return _d

def reference(L0_attn_resid, L0_attn_Wq, L0_attn_Wk, L0_attn_Wv, L0_attn_Wo, L0_ffn_gate_w, L0_ffn_base_w, L0_ffn_base_b, L0_ffn_lora_A, L0_ffn_lora_B):

    def _L0_attn_ref(resid, Wq, Wk, Wv, Wo):
        import math
        import jax, jax.numpy as jnp
        import numpy as np
        D_MODEL = 1024
        N_HEADS = 32
        N_KV_HEADS = 8
        D_HEAD = D_MODEL // N_HEADS
        GROUP = N_HEADS // N_KV_HEADS
        ROPE = dict(rope_theta=500000.0, factor=32.0, hi_freq_factor=4.0, lo_freq_factor=1.0, original_context_length=2048)

        def _rope_cos_sin(head_dim, pos, dtype):
            idx = jnp.arange(0, head_dim, 2, dtype=jnp.float32) / head_dim
            freq = 1.0 / (2.0 * math.pi) * ROPE['rope_theta'] ** (-idx)
            factor, lo, hi = (ROPE['factor'], ROPE['lo_freq_factor'], ROPE['hi_freq_factor'])
            L0 = ROPE['original_context_length']
            freq_low, freq_high = (lo / L0, hi / L0)
            freq_scaled = jnp.where(freq < freq_low, freq / factor, freq)
            smooth = jnp.clip((L0 * freq - lo) / (hi - lo), 0.0, 1.0)
            freq_smooth = (1.0 - smooth) * (freq / factor) + smooth * freq
            is_mid = (freq >= freq_low) & (freq <= freq_high)
            freq = jnp.where(is_mid, freq_smooth, freq_scaled)
            phase = 2.0 * math.pi * pos.astype(jnp.float32)[:, None] * freq[None, :]
            emb = jnp.concatenate([phase, phase], axis=-1)
            return (jnp.cos(emb).astype(dtype), jnp.sin(emb).astype(dtype))

        def _rotate_half(x):
            h = x.shape[-1] // 2
            return jnp.concatenate([-x[..., h:], x[..., :h]], axis=-1)
        B, T, _ = resid.shape
        q = (resid @ Wq).reshape(B, T, N_HEADS, D_HEAD).transpose(0, 2, 1, 3)
        k = (resid @ Wk).reshape(B, T, N_KV_HEADS, D_HEAD).transpose(0, 2, 1, 3)
        v = (resid @ Wv).reshape(B, T, N_KV_HEADS, D_HEAD).transpose(0, 2, 1, 3)
        cos, sin = _rope_cos_sin(D_HEAD, jnp.arange(T), resid.dtype)
        cos = cos[None, None]
        sin = sin[None, None]
        q = q * cos + _rotate_half(q) * sin
        k = k * cos + _rotate_half(k) * sin
        qg = q.reshape(B, N_KV_HEADS, GROUP, T, D_HEAD)
        att = jnp.einsum('bhgqd,bhkd->bhgqk', qg.astype(jnp.float32), k.astype(jnp.float32)) / math.sqrt(D_HEAD)
        causal = jnp.tril(jnp.ones((T, T), dtype=bool))
        att = jnp.where(causal[None, None, None], att, -jnp.inf)
        probs = jax.nn.softmax(att, axis=-1).astype(resid.dtype)
        ctx = jnp.einsum('bhgqk,bhkd->bhgqd', probs, v)
        out = ctx.reshape(B, N_HEADS, T, D_HEAD).transpose(0, 2, 1, 3).reshape(B, T, D_MODEL)
        return out @ Wo

    def _L0_ffn_ref(x, gate_w, base_w, base_b, lora_A, lora_B):
        import jax, jax.numpy as jnp
        import numpy as np
        B, S, D_IN, D_OUT = (2, 512, 1024, 1024)
        E, K, R = (8, 2, 16)
        SCALING = 32.0 / 16.0
        gate_logits = jnp.einsum('bsd,ed->bse', x, gate_w)
        weights, selected = jax.lax.top_k(gate_logits, K)
        weights = jax.nn.softmax(weights.astype(jnp.float32), axis=2).astype(x.dtype)
        result = jnp.einsum('bsd,od->bso', x, base_w) + base_b
        w_full = jnp.sum(jax.nn.one_hot(selected, E, dtype=x.dtype) * weights[..., None], axis=2)
        low = jnp.einsum('bsd,erd->ebsr', x, lora_A)
        lora_out = jnp.einsum('ebsr,eor,bse->bso', low, lora_B, w_full)
        result = result + SCALING * lora_out
        return result
    x = L0_attn_resid
    x = x + 0.5 * _L0_ffn_ref(_layernorm(x, axis=-1), L0_ffn_gate_w, L0_ffn_base_w, L0_ffn_base_b, L0_ffn_lora_A, L0_ffn_lora_B)
    x = x + _L0_attn_ref(_layernorm(x, axis=-1), L0_attn_Wq, L0_attn_Wk, L0_attn_Wv, L0_attn_Wo)
    x = x + 0.5 * _L0_ffn_ref(_layernorm(x, axis=-1), L0_ffn_gate_w, L0_ffn_base_w, L0_ffn_base_b, L0_ffn_lora_A, L0_ffn_lora_B)
    return x

_drawn_inputs = setup_inputs


def setup_inputs(seed=0):
    import zlib

    import numpy as np

    out = dict(_drawn_inputs(seed))
    spreads = {}
    factors = {'L0_attn_Wq': 4.614, 'L0_attn_Wk': 4.531, 'L0_ffn_base_b': 3.381}
    for name, (base, spread) in spreads.items():
        noise = np.random.default_rng([zlib.crc32(name.encode()), seed]).standard_normal(out[name].shape)
        drawn = base * np.exp(spread * noise) if base else spread * noise
        out[name] = jnp.asarray(drawn.astype(out[name].dtype))
    for name, factor in factors.items():
        out[name] = (out[name] * factor).astype(out[name].dtype)
    return out
```

```python
from contextlib import ExitStack

import numpy as np

import concourse.bass as bass
from concourse import mybir

F32 = mybir.dt.float32
F32R = mybir.dt.float32r
BF16 = mybir.dt.bfloat16
U32 = mybir.dt.uint32
ALU = mybir.AluOpType
ACT = mybir.ActivationFunctionType

P = 128
B, T, D = 2, 1024, 1024
N = B * T
KC = D // P
NT = N // P
HALF = 512
NH, NKV, DH = 32, 8, 32
G = NH // NKV
NG = B * NKV
E, R = 8, 16
ER = E * R
EPS = 1e-5
ROUTE = 10
NEG = -1.0e30


def split_products(pe, out, stat_hi, stat_lo, mov_hi, mov_lo, start, stop):
    pe.matmul(out, stat_hi, mov_hi, start=start, stop=False)
    pe.matmul(out, stat_hi, mov_lo, start=False, stop=False)
    return pe.matmul(out, stat_lo, mov_hi, start=False, stop=stop)


def wait_apart(eng, sem, value, passed):
    eng.wait_ge(sem, value)
    eng.sem_inc(passed, 1)


def ffn_stage(nc, name, x_src, x_dst, w, consts, attn=None):
    with ExitStack() as ctx:
        def sb(n, shape, dt):
            return ctx.enter_context(nc.sbuf_tensor(f"{name}_{n}", shape, dt))

        def sem(n):
            return ctx.enter_context(nc.semaphore(f"{name}_{n}"))

        wt_hi = sb("wt_hi", [P, KC, D], F32R)
        wt_lo = sb("wt_lo", [P, KC, D], F32R)
        ag_hi = sb("ag_hi", [P, KC, ER + E], F32R)
        ag_lo = sb("ag_lo", [P, KC, ER + E], F32R)
        bt_hi = sb("bt_hi", [P, D], F32R)
        bt_lo = sb("bt_lo", [P, D], F32R)
        if attn:
            wo_hi = sb("wo_hi", [P, KC, D], F32R)
            wo_lo = sb("wo_lo", [P, KC, D], F32R)
            ctxT = sb("ctxT", [P, 2, 2, KC, P], F32R)
        x_ring = sb("x_ring", [P, 4, D], F32)
        half_bias = sb("half_bias", [P, D], F32)
        h = sb("h", [P, D], F32)
        hT_hi = sb("hT_hi", [P, 2, KC, P], F32R)
        hT_lo = sb("hT_lo", [P, 2, KC, P], F32R)
        stats = sb("stats", [P, 2, 6], F32)
        mv = sb("mv", [P, 2], F32)
        std = sb("std", [P, 1], F32)
        rstd = sb("rstd", [P, 1], F32)
        eps = sb("eps", [P, 1], F32)
        top = sb("top", [P, 8], F32)
        top_idx = sb("top_idx", [P, 8], U32)
        idx_f = sb("idx_f", [P, 2], F32)
        gap = sb("gap", [P, 1], F32)
        expgap = sb("expgap", [P, 1], F32)
        onep = sb("onep", [P, 1], F32)
        w1 = sb("w1", [P, 1], F32)
        w2 = sb("w2", [P, 1], F32)
        wf1 = sb("wf1", [P, E], F32)
        wf2 = sb("wf2", [P, E], F32)
        w_full = sb("w_full", [P, E, 1], F32)
        low_s = sb("low_s", [P, ER], F32)
        lowT_hi = sb("lowT_hi", [P, P], F32R)
        lowT_lo = sb("lowT_lo", [P, P], F32R)
        ident = sb("ident", [P, P], F32)
        expert = sb("expert", [P, E], F32)

        ps = ctx.enter_context(nc.psum_tensor(f"{name}_ps", [P, 8, HALF], F32))
        turn_ps = [ps[:, 2 * i:2 * i + 2, :].rearrange("p a (c n) -> p (a c) n", n=P) for i in range(2)]
        hT_ps = turn_ps[0]
        ffn_ps = ps[:, 2:4, :]
        wo_ps = ps[:, 4:6, :]
        gl_ps = ps[:, 6, 0:ER + E]
        lowT_ps = ps[:, 7, 0:P]

        items = [("base", o) for o in range(KC)] + [("A", 0), ("B", 0), ("gate", 0)]
        if attn:
            items += [("wo", k) for k in range(KC)]
        real = range(len(items))
        turned = [i for i in real if items[i][0] != "wo"]

        def raw_loads(i):
            return 16 * sum(1 for j in real if j % 4 == i % 4 and j <= i and items[j][0] != "B")

        slot_loads = [raw_loads(max(i for i in real if i % 4 == s)) for s in range(4)]

        x_loaded = [sem(f"x_loaded{s}") for s in range(4)]
        ctx_loaded = [sem(f"ctx_loaded{s}") for s in range(2)]
        passed = sem("passed")
        const_loaded = sem("const_loaded")
        CONSTS = 2 * 16
        eps_set = sem("eps_set")
        bias_loaded = sem("bias_loaded")
        b_loaded = sem("b_loaded")
        raw_turned = sem("raw_turned")
        w_hi_done = sem("w_hi_done")
        w_lo_done = sem("w_lo_done")
        ln_step = sem("ln_step")
        std_ready = sem("std_ready")
        h_ready = sem("h_ready")
        h_turned = sem("h_turned")
        hT_hi_done = sem("hT_hi_done")
        hT_lo_done = sem("hT_lo_done")
        gl_done = sem("gl_done")
        route = sem("route")
        exp_done = sem("exp_done")
        low_ready = sem("low_ready")
        low_turned = sem("low_turned")
        lowT_hi_done = sem("lowT_hi_done")
        lowT_lo_done = sem("lowT_lo_done")
        ffn_done = sem("ffn_done")
        ffn_added = sem("ffn_added")
        bias_ready = sem("bias_ready")
        bias_added = sem("bias_added")
        wo_done = sem("wo_done")
        wo_added = sem("wo_added")
        stored = [sem(f"stored{s}") for s in range(4)]

        def x_wait(eng, i, u):
            eng.wait_ge(x_loaded[u % 4], (i + u // 4) * 16 + (slot_loads[u % 4] + 16))

        def load_x(eng, t, s):
            eng.dma_start(x_ring[:, s, :], x_src[bass.ds(t * P, P), :]).then_inc(x_loaded[s], 16)

        def load_ctx(eng, t, par):
            for part, src in enumerate((attn["ctx_hi"], attn["ctx_lo"])):
                eng.dma_start(ctxT[:, par, part, :, :].bitcast(F32), src[bass.ds(t, 1), :, :, :].rearrange("t c p n -> p (t c) n")).then_inc(ctx_loaded[par], 16)

        def run_tiles(eng, step):
            with eng.Fori(0, NT // 4 - 1, 1) as i:
                for u in range(4):
                    step(i, 4 * i + u, u, 3)
            for u in range(4):
                step(NT // 4 - 1, NT - 4 + u, u, 3 - u)

        def turned_view(n, kind):
            v = turn_ps[n % 2]
            return v[:, :, 0:E] if kind == "gate" else v

        def weight_view(kind, k, part):
            if kind == "base":
                return (wt_hi, wt_lo)[part][:, :, k * P:(k + 1) * P]
            if kind == "A":
                return (ag_hi, ag_lo)[part][:, :, 0:ER]
            if kind == "gate":
                return (ag_hi, ag_lo)[part][:, :, ER:ER + E]
            if kind == "B":
                return (bt_hi, bt_lo)[part][:, :].rearrange("p (c n) -> p c n", n=P)
            return (wo_hi, wo_lo)[part][:, k, :]

        block = ctx.enter_context(nc.Block())

        @block.sync
        def _(sp):
            sp.dma_start(ident[:], consts["identity"]).then_inc(const_loaded, 16)
            sp.dma_start(expert[:], consts["expert"]).then_inc(const_loaded, 16)
            sp.dma_start(half_bias[:], w["base_b"].rearrange("(a n) -> a n", a=1).broadcast_to([P, D])).then_inc(bias_loaded, 16)
            for i in real:
                kind, k = items[i]
                s = i % 4
                if i >= 4:
                    if items[i - 4][0] == "wo":
                        sp.wait_ge(w_lo_done, i - 4 + 1)
                    else:
                        sp.wait_ge(raw_turned, turned.index(i - 4) + 1)
                src = {"base": lambda: w["base_w"][k * P:(k + 1) * P, :],
                       "A": lambda: w["lora_A"].rearrange("e r d -> (e r) d"),
                       "gate": lambda: w["gate_w"],
                       "wo": lambda: attn["wo"][k * P:(k + 1) * P, :]}
                if kind == "B":
                    with nc.allow_non_contiguous_dma("64-byte runs of lora_B"):
                        for e in range(E):
                            dst = x_ring[:, s, :].rearrange("p (c e r) -> p c e r", e=E, r=R)[:, :, e, :]
                            ins = sp.dma_start(dst, w["lora_B"][e].rearrange("(c p) r -> p c r", p=P))
                            ins.then_inc(b_loaded, 16)
                elif kind == "gate":
                    sp.dma_start(x_ring[0:E, s, :], src[kind]()).then_inc(x_loaded[s], 16)
                else:
                    sp.dma_start(x_ring[:, s, :], src[kind]()).then_inc(x_loaded[s], 16)
            sp.wait_ge(raw_turned, len(turned))
            sp.wait_ge(w_lo_done, len(real))
            sp.dma_start(x_ring[:, 0, :], x_src[0:P, :]).then_inc(x_loaded[0], 16)
            if attn:
                load_ctx(sp, 0, 0)
            for t in range(1, 3):
                sp.dma_start(x_ring[:, t, :], x_src[t * P:(t + 1) * P, :]).then_inc(x_loaded[t], 16)
                if attn and t < 2:
                    load_ctx(sp, t, t)

            def step(i, t, u, more):
                if attn and more >= 2:
                    sp.wait_ge(wo_done, 2 * t + 2)
                    load_ctx(sp, t + 2, u % 2)
                if more >= 3:
                    s = (u + 3) % 4
                    sp.wait_ge(stored[s], (i + (u + 3) // 4) * 16 + (16 if s == 3 else 0))
                    load_x(sp, t + 3, s)
                sp.wait_ge(ffn_added, 2 * t + 4)
                sp.dma_start(x_dst[bass.ds(t * P, P), :], x_ring[:, u, :]).then_inc(stored[u], 16)
            run_tiles(sp, step)
            for s in range(4):
                sp.wait_ge(stored[s], 16 * (NT // 4) + (16 if s == 3 else 0))

        @block.gpsimd
        def _(pool):
            pool.memset(eps[:], EPS).then_inc(eps_set, 1)
            pool.sem_inc(stored[3], 16)
            pool.wait_ge(bias_loaded, 16)
            pool.tensor_scalar(half_bias[:], half_bias[:], 0.5, None, ALU.mult).then_inc(bias_ready, 1)
            pool.wait_ge(bias_ready, 1)
            with pool.Fori(0, NT // 4, 1) as i:
                for u in range(4):
                    pool.wait_ge(h_ready, 4 * i + u + 1)
                    pool.tensor_tensor(x_ring[:, u, :], x_ring[:, u, :], half_bias[:], ALU.add).then_inc(bias_added, 1)

        @block.tensor
        def _(pe):
            pe.sem_inc(ffn_added, 2)
            pe.sem_inc(low_turned, 1)
            pe.sem_inc(ffn_done, 1)
            if attn:
                pe.sem_inc(wo_added, 2)
            pe.wait_ge(const_loaded, CONSTS)
            for n, i in enumerate(turned):
                kind, k = items[i]
                s = i % 4
                if kind == "B":
                    pe.wait_ge(b_loaded, 16 * E)
                else:
                    pe.wait_ge(x_loaded[s], raw_loads(i))
                if n >= 2:
                    pe.wait_ge(w_lo_done, n - 1)
                out = turn_ps[n % 2]
                for c in range(KC):
                    if kind == "gate":
                        last = pe.transpose(out[:, c, 0:E], x_ring[0:E, s, c * P:(c + 1) * P], ident[0:E, 0:E])
                    else:
                        last = pe.transpose(out[:, c, :], x_ring[:, s, c * P:(c + 1) * P], ident[:])
                last.then_inc(raw_turned, 1)
            pe.wait_ge(w_lo_done, len(real))

            def turn_h(t):
                pe.wait_ge(h_ready, t + 1)
                pe.wait_ge(hT_lo_done, t)
                for c in range(KC):
                    last = pe.transpose(hT_ps[:, c, :], h[:, c * P:(c + 1) * P], ident[:])
                last.then_inc(h_turned, 1)

            def low_and_gate(t, par):
                pe.wait_ge(hT_lo_done, t + 1)
                pe.wait_ge(low_ready, t)
                for c in range(KC):
                    last = split_products(pe, gl_ps, hT_hi[:, par, c, :], hT_lo[:, par, c, :],
                                          ag_hi[:, c, :], ag_lo[:, c, :], c == 0, c == KC - 1)
                last.then_inc(gl_done, 1)

            def base(t, par, half):
                pe.wait_ge(ffn_added, 2 * t + half + 1)
                cols = slice(half * HALF, (half + 1) * HALF)
                for c in range(KC):
                    split_products(pe, ffn_ps[:, half, :], hT_hi[:, par, c, :], hT_lo[:, par, c, :],
                                   wt_hi[:, c, cols], wt_lo[:, c, cols], c == 0, False)

            def turn_low(t):
                pe.wait_ge(low_ready, t + 1)
                pe.transpose(lowT_ps, low_s[:], ident[:]).then_inc(low_turned, 1)

            def lora(t):
                pe.wait_ge(lowT_lo_done, t + 1)
                for half in range(2):
                    cols = slice(half * HALF, (half + 1) * HALF)
                    split_products(pe, ffn_ps[:, half, :], lowT_hi[:], lowT_lo[:], bt_hi[:, cols], bt_lo[:, cols],
                                   False, True).then_inc(ffn_done, 1)

            def project(t, u):
                par = u % 2
                pe.wait_ge(ctx_loaded[par], 32 * (t // 2) + 32)
                for half in range(2):
                    pe.wait_ge(wo_added, 2 * t + half + 1)
                    cols = slice(half * HALF, (half + 1) * HALF)
                    for c in range(KC):
                        last = split_products(pe, wo_ps[:, half, :], ctxT[:, par, 0, c, :], ctxT[:, par, 1, c, :],
                                              wo_hi[:, c, cols], wo_lo[:, c, cols], c == 0, c == KC - 1)
                    last.then_inc(wo_done, 1)

            if attn:
                project(0, 0)
                project(1, 1)
            turn_h(0)
            low_and_gate(0, 0)

            def step(i, t, u, more):
                if more >= 1:
                    turn_h(t + 1)
                base(t, u % 2, 0)
                turn_low(t)
                if attn and more >= 2:
                    project(t + 2, u + 2)
                base(t, u % 2, 1)
                lora(t)
                if more >= 1:
                    low_and_gate(t + 1, (u + 1) % 2)
            run_tiles(pe, step)

        @block.scalar
        def _(act):
            for n, i in enumerate(real):
                kind, k = items[i]
                scale = 0.5 if kind == "base" else 1.0
                if kind == "wo":
                    act.wait_ge(x_loaded[i % 4], raw_loads(i))
                    src = x_ring[:, i % 4, :]
                else:
                    act.wait_ge(raw_turned, turned.index(i) + 1)
                    src = turned_view(n, kind)
                act.activation(weight_view(kind, k, 0), src, ACT.Copy, scale=scale).then_inc(w_hi_done, 1)

            def high_hT(t, par):
                act.wait_ge(h_turned, t + 1)
                act.activation(hT_hi[:, par, :, :], hT_ps, ACT.Copy).then_inc(hT_hi_done, 1)

            def deviation(t):
                act.wait_ge(ln_step, 4 * t + 3)
                act.activation(std[:], mv[:, 1:2], ACT.Sqrt, bias=eps[:, 0:1]).then_inc(std_ready, 1)

            act.wait_ge(eps_set, 1)
            deviation(0)
            high_hT(0, 0)
            deviation(1)

            def step(i, t, u, more):
                act.wait_ge(route, ROUTE * t + 3)
                act.activation(expgap[:], gap[:], ACT.Exp).then_inc(exp_done, 1)
                act.wait_ge(ffn_done, 2 * t + 1)
                if more >= 1:
                    high_hT(t + 1, (u + 1) % 2)
                act.wait_ge(low_turned, t + 2)
                act.activation(lowT_hi[:], lowT_ps, ACT.Copy).then_inc(lowT_hi_done, 1)
                if more >= 2:
                    deviation(t + 2)
            run_tiles(act, step)

        @block.vector
        def _(dve):
            for n, i in enumerate(real):
                kind, k = items[i]
                scale = 0.5 if kind == "base" else 1.0
                src = x_ring[:, i % 4, :] if kind == "wo" else turned_view(n, kind)
                dve.wait_ge(w_hi_done, n + 1)
                if kind == "base":
                    for c in range(0, KC, 4):
                        last = dve.scalar_tensor_tensor(weight_view(kind, k, 1)[:, c:c + 4, :], src[:, c:c + 4, :], 0.5,
                                                 weight_view(kind, k, 0)[:, c:c + 4, :].bitcast(F32), ALU.mult, ALU.subtract)
                    last.then_inc(w_lo_done, 1)
                else:
                    dve.tensor_tensor(weight_view(kind, k, 1), src, weight_view(kind, k, 0).bitcast(F32),
                                      ALU.subtract).then_inc(w_lo_done, 1)

            def layer_norm(i, t, u):
                x = x_ring[:, u % 4, :]
                if attn is None:
                    x_wait(dve, i, u)
                else:
                    dve.wait_ge(wo_added, 2 * t + 4)
                for half in range(2):
                    dve.bn_stats(stats[:, half, :], x[:, half * HALF:(half + 1) * HALF]).then_inc(ln_step, 1)
                wait_apart(dve, ln_step, 4 * t + 2, passed)
                dve.bn_aggr(mv[:], stats[:, :, :].rearrange("p a b -> p (a b)")).then_inc(ln_step, 1)
                dve.wait_ge(std_ready, t + 1)
                dve.reciprocal(rstd[:], std[:]).then_inc(ln_step, 1)
                dve.wait_ge(ln_step, 4 * t + 4)
                dve.wait_ge(h_turned, t)
                dve.tensor_scalar(h[:], x, mv[:, 0:1], rstd[:, 0:1], ALU.subtract, ALU.mult).then_inc(h_ready, 1)

            def low_hT(t, par):
                dve.wait_ge(hT_hi_done, t + 1)
                dve.tensor_tensor(hT_lo[:, par, :, :], hT_ps, hT_hi[:, par, :, :].bitcast(F32),
                                  ALU.subtract).then_inc(hT_lo_done, 1)

            def routing(t):
                logits = gl_ps[:, ER:ER + E]
                wait_apart(dve, gl_done, t + 1, passed)
                dve.max(top[:], logits).then_inc(route, 1)
                wait_apart(dve, route, ROUTE * t + 1, passed)
                dve.max_index(top_idx[:], top[:], logits).then_inc(route, 1)
                dve.tensor_tensor(gap[:], top[:, 1:2], top[:, 0:1], ALU.subtract).then_inc(route, 1)
                dve.wait_ge(route, ROUTE * t + 3)
                dve.tensor_copy(idx_f[:], top_idx[:, 0:2]).then_inc(route, 1)
                dve.wait_ge(exp_done, t + 1)
                dve.tensor_scalar(onep[:], expgap[:], 1.0, None, ALU.add).then_inc(route, 1)
                dve.wait_ge(route, ROUTE * t + 5)
                dve.reciprocal(w1[:], onep[:]).then_inc(route, 1)
                dve.wait_ge(route, ROUTE * t + 6)
                dve.tensor_tensor(w2[:], expgap[:], w1[:], ALU.mult).then_inc(route, 1)
                dve.tensor_scalar(wf1[:], expert[:], idx_f[:, 0:1], w1[:, 0:1], ALU.is_equal, ALU.mult).then_inc(route, 1)
                dve.wait_ge(route, ROUTE * t + 8)
                dve.tensor_scalar(wf2[:], expert[:], idx_f[:, 1:2], w2[:, 0:1], ALU.is_equal, ALU.mult).then_inc(route, 1)
                dve.wait_ge(route, ROUTE * t + 9)
                dve.tensor_tensor(w_full[:, :, 0], wf1[:], wf2[:], ALU.add).then_inc(route, 1)
                dve.wait_ge(route, ROUTE * t + 10)
                dve.wait_ge(low_turned, t + 1)
                dve.tensor_tensor(low_s[:].rearrange("p (e r) -> p e r", r=R),
                                  gl_ps[:, 0:ER].rearrange("p (e r) -> p e r", r=R),
                                  w_full[:].broadcast_to([P, E, R]), ALU.mult).then_inc(low_ready, 1)

            def add_projection(i, t, u):
                x_wait(dve, i, u)
                for half in range(2):
                    cols = slice(half * HALF, (half + 1) * HALF)
                    dve.wait_ge(wo_done, 2 * t + half + 1)
                    dve.tensor_tensor(x_ring[:, u % 4, cols], wo_ps[:, half, :], x_ring[:, u % 4, cols],
                                      ALU.add).then_inc(wo_added, 1)

            dve.wait_ge(const_loaded, CONSTS)
            if attn:
                add_projection(0, 0, 0)
            layer_norm(0, 0, 0)
            low_hT(0, 0)
            if attn:
                add_projection(0, 1, 1)
            layer_norm(0, 1, 1)

            def step(i, t, u, more):
                routing(t)
                if more >= 1:
                    low_hT(t + 1, (u + 1) % 2)
                dve.wait_ge(lowT_hi_done, t + 1)
                dve.tensor_tensor(lowT_lo[:], lowT_ps, lowT_hi[:].bitcast(F32), ALU.subtract).then_inc(lowT_lo_done, 1)
                if more >= 2:
                    if attn:
                        add_projection(i, t + 2, u + 2)
                    layer_norm(i, t + 2, u + 2)
                dve.wait_ge(bias_added, t + 1)
                for half in range(2):
                    cols = slice(half * HALF, (half + 1) * HALF)
                    dve.wait_ge(ffn_done, 2 * t + (half + 2))
                    dve.tensor_tensor(x_ring[:, u, cols], ffn_ps[:, half, :], x_ring[:, u, cols],
                                      ALU.add).then_inc(ffn_added, 1)
            run_tiles(dve, step)


def qkv_stage(nc, x_src, w, consts, scr):
    NCH = T // HALF
    TC = HALF // P
    KV = NKV * DH
    NO = KC + KV // P
    with ExitStack() as ctx:
        def sb(n, shape, dt):
            return ctx.enter_context(nc.sbuf_tensor(f"qkv_{n}", shape, dt))

        def sem(n):
            return ctx.enter_context(nc.semaphore(f"qkv_{n}"))

        wq_hi = sb("wq_hi", [P, KC, D], F32R)
        wq_lo = sb("wq_lo", [P, KC, D], F32R)
        wkv_hi = sb("wkv_hi", [P, KC, 2 * KV], F32R)
        wkv_lo = sb("wkv_lo", [P, KC, 2 * KV], F32R)
        hT_hi = sb("hT_hi", [P, NCH, KC, HALF], F32R)
        hT_lo = sb("hT_lo", [P, NCH, KC, HALF], F32R)
        x_ring = sb("x_ring", [P, 2, D], F32)
        h = sb("h", [P, D], F32)
        stats = sb("stats", [P, 2, 6], F32)
        mv = sb("mv", [P, 2], F32)
        std = sb("std", [P, 1], F32)
        rstd = sb("rstd", [P, 1], F32)
        eps = sb("eps", [P, 1], F32)
        cos = sb("cos", [P, T], F32)
        sin = sb("sin", [P, T], F32)
        rot = sb("rot", [P, 2, HALF], F32)
        rope = sb("rope", [P, 2, HALF], F32)
        rope_hi = sb("rope_hi", [P, 2, HALF], F32R)
        rope_lo = sb("rope_lo", [P, 2, HALF], F32R)
        v_out = sb("v_out", [P, 2, KV], F32)
        ident = sb("ident", [P, P], F32)

        ps = ctx.enter_context(nc.psum_tensor("qkv_ps", [P, 8, HALF], F32))
        hT_ps = ps[:, 0:2, :].rearrange("p a (c n) -> p (a c) n", n=P)

        w_loaded = [sem(f"w_loaded{s}") for s in range(2)]
        x_loaded = [sem(f"x_loaded{s}") for s in range(2)]
        passed = sem("passed")
        const_loaded = sem("const_loaded")
        CONSTS = 3 * 16
        eps_set = sem("eps_set")
        w_hi_done = sem("w_hi_done")
        w_lo_done = sem("w_lo_done")
        ln_step = sem("ln_step")
        std_ready = sem("std_ready")
        h_ready = sem("h_ready")
        h_turned = sem("h_turned")
        hT_hi_done = sem("hT_hi_done")
        hT_lo_done = sem("hT_lo_done")
        proj_done = sem("proj_done")
        cos_done = sem("cos_done")
        swapped = sem("swapped")
        sin_done = sem("sin_done")
        rope_done = sem("rope_done")
        hi_done = sem("hi_done")
        lo_done = sem("lo_done")
        out_stored = [sem(f"out_stored{s}") for s in range(2)]
        v_done = sem("v_done")
        v_copied = sem("v_copied")
        v_stored = [sem(f"v_stored{s}") for s in range(2)]

        witems = [("q", k) for k in range(KC)] + [("kv", k) for k in range(KC)]
        q_rows = scr["q_hi"].rearrange("n r t -> (n r) t"), scr["q_lo"].rearrange("n r t -> (n r) t")
        k_rows = scr["k_hi"].rearrange("n r t -> (n r) t"), scr["k_lo"].rearrange("n r t -> (n r) t")

        block = ctx.enter_context(nc.Block())

        def wide(kind):
            return D if kind == "q" else 2 * KV

        @block.sync
        def _(sp):
            sp.dma_start(ident[:], consts["identity"]).then_inc(const_loaded, 16)
            sp.dma_start(cos[:], consts["rope_cos"]).then_inc(const_loaded, 16)
            sp.dma_start(sin[:], consts["rope_sin"]).then_inc(const_loaded, 16)
            for n, (kind, k) in enumerate(witems):
                if n >= 2:
                    sp.wait_ge(w_lo_done, n - 1)
                rows = slice(k * P, (k + 1) * P)
                if kind == "q":
                    sp.dma_start(x_ring[:, n % 2, :], w["Wq"][rows, :]).then_inc(w_loaded[n % 2], 16)
                else:
                    sp.dma_start(x_ring[:, n % 2, 0:KV], w["Wk"][rows, :]).then_inc(w_loaded[n % 2], 16)
                    sp.dma_start(x_ring[:, n % 2, KV:2 * KV], w["Wv"][rows, :]).then_inc(w_loaded[n % 2], 16)
            sp.wait_ge(w_lo_done, len(witems))
            with sp.Fori(0, B, 1) as b:
                for t in range(NCH * TC):
                    sp.wait_ge(h_ready, b * (NCH * TC) + (t + 1))
                    sp.dma_start(x_ring[:, t % 2, :], x_src[bass.ds(b * T + t * P, P), :]).then_inc(x_loaded[t % 2], 16)

        @block.tensor
        def _(pe):
            pe.sem_inc(h_ready, 2)
            pe.sem_inc(cos_done, 4)
            pe.sem_inc(rope_done, 2)
            pe.sem_inc(lo_done, 2)
            pe.sem_inc(v_copied, 2)
            for first_free in (hT_lo_done, h_turned, v_done):
                pe.sem_inc(first_free, 1)
            for first_free in out_stored + v_stored:
                pe.sem_inc(first_free, 16)
            pe.wait_ge(const_loaded, CONSTS)

            def turn_h(b, t):
                tile = b * (NCH * TC) + t
                pe.wait_ge(h_ready, tile + 3)
                pe.wait_ge(hT_lo_done, tile + 1)
                for c in range(KC):
                    last = pe.transpose(hT_ps[:, c, :], h[:, c * P:(c + 1) * P], ident[:])
                last.then_inc(h_turned, 1)

            with pe.Fori(0, B, 1) as b:
                for t in range(TC):
                    turn_h(b, t)
                for ch in range(NCH):
                    pe.wait_ge(hT_lo_done, b * (NCH * TC) + ((ch + 1) * TC + 1))
                    for o in range(NO):
                        g = ch * NO + o
                        pe.wait_ge(cos_done, b * (NCH * NO) + (g + 1))
                        wh, wl = (wq_hi, wq_lo) if o < KC else (wkv_hi, wkv_lo)
                        cols = slice((o % KC) * P, (o % KC + 1) * P)
                        for c in range(KC):
                            last = split_products(pe, ps[:, 2 + g % 4, :], wh[:, c, cols], wl[:, c, cols],
                                                  hT_hi[:, ch, c, :], hT_lo[:, ch, c, :], c == 0, c == KC - 1)
                        last.then_inc(proj_done, 1)
                        if ch + 1 < NCH and o % 2 == 1 and o // 2 < TC:
                            turn_h(b, (ch + 1) * TC + o // 2)
                    for s in range(TC):
                        t = ch * TC + s
                        pe.wait_ge(v_copied, b * (NCH * TC) + (t + 1))
                        for c in range(KC):
                            tok = slice(s * P, (s + 1) * P)
                            last = split_products(pe, ps[:, 6 + t % 2, 0:KV], hT_hi[:, ch, c, tok], hT_lo[:, ch, c, tok],
                                                  wkv_hi[:, c, KV:2 * KV], wkv_lo[:, c, KV:2 * KV], c == 0, c == KC - 1)
                        last.then_inc(v_done, 1)

        @block.scalar
        def _(act):
            for n, (kind, k) in enumerate(witems):
                count = 16 * (n // 2 + 1) if n < KC else 16 * (KC // 2) + 32 * ((n - KC) // 2 + 1)
                act.wait_ge(w_loaded[n % 2], count)
                dst = wq_hi[:, k, :] if kind == "q" else wkv_hi[:, k, :]
                act.activation(dst, x_ring[:, n % 2, 0:wide(kind)], ACT.Copy).then_inc(w_hi_done, 1)

            def deviation(b, t):
                act.wait_ge(ln_step, b * (4 * NCH * TC) + (4 * t + 3))
                act.activation(std[:], mv[:, 1:2], ACT.Sqrt, bias=eps[:, 0:1]).then_inc(std_ready, 1)

            def high_hT(b, t):
                tile = b * (NCH * TC) + t
                act.wait_ge(h_turned, tile + 2)
                act.activation(hT_hi[:, t // TC, :, (t % TC) * P:(t % TC + 1) * P], hT_ps, ACT.Copy).then_inc(hT_hi_done, 1)

            def high_out(b, g):
                act.wait_ge(rope_done, b * (NCH * NO) + (g + 3))
                act.wait_ge(out_stored[g % 2], b * (NCH * NO * 16) + (g // 2) * 32 + 16)
                act.activation(rope_hi[:, g % 2, :], rope[:, g % 2, :], ACT.Copy).then_inc(hi_done, 1)

            def store_out(b, g):
                ch, o = g // NO, g % NO
                cols = slice(ch * HALF, (ch + 1) * HALF)
                act.wait_ge(hi_done, b * (NCH * NO) + (g + 1))
                act.wait_ge(lo_done, b * (NCH * NO) + (g + 3))
                for part, buf in enumerate((rope_hi, rope_lo)):
                    rows = q_rows[part][bass.ds(b * (NKV * P) + o * P, P), cols] if o < KC \
                        else k_rows[part][bass.ds(b * KV + (o - KC) * P, P), cols]
                    act.dma_start(rows, buf[:, g % 2, :].bitcast(F32)).then_inc(out_stored[g % 2], 16)

            def store_v(b, t):
                act.wait_ge(v_copied, b * (NCH * TC) + (t + 3))
                dst = scr["v"][bass.ds(b * NKV, NKV), t * P:(t + 1) * P, :].rearrange("n t d -> t n d")
                act.dma_start(dst, v_out[:, t % 2, :].rearrange("p (n d) -> p n d", d=DH)).then_inc(v_stored[t % 2], 16)

            act.wait_ge(eps_set, 1)
            with act.Fori(0, B, 1) as b:
                act.wait_ge(v_done, b * (NCH * TC) + 1)
                for t in range(TC):
                    deviation(b, t)
                    high_hT(b, t)
                for ch in range(NCH):
                    for o in range(NO):
                        g = ch * NO + o
                        if ch + 1 < NCH and o % 2 == 0 and o // 2 < TC:
                            deviation(b, (ch + 1) * TC + o // 2)
                        if o >= 1:
                            high_out(b, g - 1)
                        if o >= 2:
                            store_out(b, g - 2)
                        if ch + 1 < NCH and o % 2 == 1 and o // 2 < TC:
                            high_hT(b, (ch + 1) * TC + o // 2)
                    high_out(b, ch * NO + NO - 1)
                    store_out(b, ch * NO + NO - 2)
                    store_out(b, ch * NO + NO - 1)
                    for s in range(TC):
                        t = ch * TC + s
                        act.wait_ge(v_done, b * (NCH * TC) + (t + 2))
                        act.wait_ge(v_stored[t % 2], b * (NCH * TC * 8) + (t // 2) * 16 + 16)
                        act.activation(v_out[:, t % 2, :], ps[:, 6 + t % 2, 0:KV], ACT.Copy).then_inc(v_copied, 1)
                        store_v(b, t)
            for s in range(2):
                act.wait_ge(out_stored[s], B * NCH * NO * 16 + 16)
                act.wait_ge(v_stored[s], B * NCH * TC * 8 + 16)

        @block.gpsimd
        def _(pool):
            pool.memset(eps[:], EPS).then_inc(eps_set, 1)
            pool.wait_ge(const_loaded, CONSTS)

            def low_part(b, g):
                pool.wait_ge(hi_done, b * (NCH * NO) + (g + 1))
                pool.tensor_tensor(rope_lo[:, g % 2, :], rope[:, g % 2, :], rope_hi[:, g % 2, :].bitcast(F32),
                                   ALU.subtract).then_inc(lo_done, 1)

            with pool.Fori(0, B, 1) as b:
                for g in range(NCH * NO):
                    cols = slice((g // NO) * HALF, (g // NO + 1) * HALF)
                    pool.wait_ge(swapped, b * (NCH * NO) + (g + 1))
                    pool.tensor_tensor(rot[:, g % 2, :], rot[:, g % 2, :], sin[:, cols], ALU.mult).then_inc(sin_done, 1)
                    if g % NO >= 1:
                        low_part(b, g - 1)
                    if g % NO == NO - 1:
                        low_part(b, g)

        @block.vector
        def _(dve):
            for n, (kind, k) in enumerate(witems):
                hi, lo = (wq_hi, wq_lo) if kind == "q" else (wkv_hi, wkv_lo)
                dve.wait_ge(w_hi_done, n + 1)
                dve.tensor_tensor(lo[:, k, :], x_ring[:, n % 2, 0:wide(kind)], hi[:, k, :].bitcast(F32),
                                  ALU.subtract).then_inc(w_lo_done, 1)

            def layer_norm(b, t):
                tile = b * (NCH * TC) + t
                x = x_ring[:, t % 2, :]
                dve.wait_ge(x_loaded[t % 2], b * (NCH * TC * 8) + 16 * (t // 2 + 1))
                for half in range(2):
                    dve.bn_stats(stats[:, half, :], x[:, half * HALF:(half + 1) * HALF]).then_inc(ln_step, 1)
                wait_apart(dve, ln_step, 4 * tile + 2, passed)
                dve.bn_aggr(mv[:], stats[:, :, :].rearrange("p a b -> p (a b)")).then_inc(ln_step, 1)
                dve.wait_ge(std_ready, tile + 1)
                dve.reciprocal(rstd[:], std[:]).then_inc(ln_step, 1)
                dve.wait_ge(ln_step, 4 * tile + 4)
                dve.wait_ge(h_turned, tile + 1)
                dve.tensor_scalar(h[:], x, mv[:, 0:1], rstd[:, 0:1], ALU.subtract, ALU.mult).then_inc(h_ready, 1)

            def low_hT(b, t):
                at = (slice(None), t // TC, slice(None), slice((t % TC) * P, (t % TC + 1) * P))
                dve.wait_ge(hT_hi_done, b * (NCH * TC) + (t + 1))
                dve.tensor_tensor(hT_lo[at], hT_ps, hT_hi[at].bitcast(F32), ALU.subtract).then_inc(hT_lo_done, 1)

            def rope_sum(b, g):
                dve.wait_ge(sin_done, b * (NCH * NO) + (g + 1))
                dve.wait_ge(cos_done, b * (NCH * NO) + (g + 5))
                dve.tensor_tensor(rope[:, g % 2, :], rope[:, g % 2, :], rot[:, g % 2, :], ALU.add).then_inc(rope_done, 1)

            swap = [(i + DH // 2) % DH for i in range(DH)]
            dve.wait_ge(const_loaded, CONSTS)
            with dve.Fori(0, B, 1) as b:
                for t in range(TC):
                    layer_norm(b, t)
                    low_hT(b, t)
                for ch in range(NCH):
                    cols = slice(ch * HALF, (ch + 1) * HALF)
                    for o in range(NO):
                        g = ch * NO + o
                        bank = ps[:, 2 + g % 4, :]
                        if ch + 1 < NCH and o % 2 == 0 and o // 2 < TC:
                            layer_norm(b, (ch + 1) * TC + o // 2)
                        dve.wait_ge(proj_done, b * (NCH * NO) + (g + 1))
                        wait_apart(dve, rope_done, b * (NCH * NO) + (g + 1), passed)
                        dve.stream_shuffle(rot[:, g % 2, :], bank, swap).then_inc(swapped, 1)
                        dve.wait_ge(lo_done, b * (NCH * NO) + (g + 1))
                        dve.tensor_tensor(rope[:, g % 2, :], bank, cos[:, cols], ALU.mult).then_inc(cos_done, 1)
                        if o >= 1:
                            rope_sum(b, g - 1)
                        if ch + 1 < NCH and o % 2 == 1 and o // 2 < TC:
                            low_hT(b, (ch + 1) * TC + o // 2)
                    rope_sum(b, ch * NO + NO - 1)


def attention_stage(nc, consts, scr):
    NQ = T // P
    QH = NQ // 2
    RING = 3
    KROWS = 3 * DH
    SCALE = float(DH) ** -0.5
    with ExitStack() as ctx:
        def sb(n, shape, dt):
            return ctx.enter_context(nc.sbuf_tensor(f"at_{n}", shape, dt))

        def sem(n):
            return ctx.enter_context(nc.semaphore(f"at_{n}"))

        qs = sb("qs", [KROWS + 2, RING, G, T], F32R)
        ks = sb("ks", [KROWS + 2, RING, T], F32R)
        vs = sb("vs", [P, RING, NQ, DH], F32)
        ones = sb("ones", [P, DH], F32)
        probs = sb("probs", [P, 3, G, HALF], F32)
        row_max = sb("row_max", [P, 2, G, QH], F32)
        neg_hi = sb("neg_hi", [G * QH, 2, P], F32R)
        neg_lo = sb("neg_lo", [G * QH, 2, P], F32R)
        score_mask = sb("score_mask", [P, T], F32)
        prob_mask_f = sb("prob_mask_f", [P, P], F32)
        prob_mask = sb("prob_mask", [P, P], BF16)
        ident = sb("ident", [P, P], F32)
        ident_b = sb("ident_b", [P, P], BF16)
        recip = sb("recip", [P, HALF], F32)
        ctxn = sb("ctxn", [P, 2, HALF], F32)
        ctx_hi = sb("ctx_hi", [P, 2, HALF], F32R)
        ctx_lo = sb("ctx_lo", [P, 2, HALF], F32R)

        ps = ctx.enter_context(nc.psum_tensor("at_ps", [P, 8, HALF], F32))
        ctx_ps = ps[:, 6, :]
        sum_ps = ps[:, 7, :]

        stacks_loaded = [sem(f"stacks_loaded{r}") for r in range(RING)]
        passed = sem("passed")
        const_loaded = sem("const_loaded")
        CONSTS = 3 * 16
        eps_set = sem("eps_set")
        const_ready = sem("const_ready")
        slot_filled = sem("slot_filled")
        slot_read = sem("slot_read")
        neg_hi_done = sem("neg_hi_done")
        rows_loaded = [sem(f"rows_loaded{h}") for h in range(2)]
        scores_done = sem("scores_done")
        exp_done = sem("exp_done")
        unit_done = sem("unit_done")
        recip_done = sem("recip_done")
        ctxn_done = sem("ctxn_done")
        chi_done = sem("chi_done")
        clo_done = sem("clo_done")
        ctx_stored = [sem(f"ctx_stored{h}") for h in range(2)]

        units = [(half, j) for half in range(2) for j in range(QH * (half + 1))]
        NU = len(units)

        def queries(u):
            half, j = units[u]
            return max(half * HALF, j * P), (half + 1) * HALF

        rows = [("row", i, g) for i in range(NQ) for g in range(G)]
        at_a = QH * G + 4
        first = rows[:at_a] + [("turn", 0, 0)] + rows[at_a:]
        weight = [(it[1] + 1) * P + 150 if it[0] == "row" else 200 for it in first]
        room = [queries(u // 2)[1] - queries(u // 2)[0] + 200 for u in range(2 * NU)]
        places = [[] for _ in range(2 * NU)]
        done, at = 0.0, 0
        for it, wgt in zip(first, weight):
            while at < 2 * NU - 1 and sum(room[:at + 1]) / sum(room) < (done + wgt / 2) / sum(weight):
                at += 1
            places[at].append(it)
            done += wgt
        places[2].insert(0, ("turn", 1, 0))
        SEQ = len(first) + 1
        PRE = len(first)
        assert SEQ % 2 == 0 and len(places[0]) + len(places[1]) >= 1

        def place_items(k, more):
            def kept(pl):
                return [it for it in pl if more or it == ("turn", 1, 0)]
            start = sum(len(kept(pl)) for pl in places[:k])
            return [(start + x, it) for x, it in enumerate(kept(places[k]))]

        def turn_position(half, more):
            return next(p for k in range(2 * NU) for p, it in place_items(k, more) if it == ("turn", half, 0))

        q_src = [scr[k].rearrange("n (g d) t -> n d g t", d=DH) for k in ("q_hi", "q_lo")]

        block = ctx.enter_context(nc.Block())

        def steps(eng, step):
            with eng.Fori(0, NG // RING - 1, 1) as i:
                for r in range(RING):
                    step(i, RING * i + r, r, 2)
            for n in range(RING * (NG // RING - 1), NG):
                step(n // RING, n, n % RING, min(NG - 1 - n, 2))

        @block.sync
        def _(sp):
            for dst, k in ((ident, "identity"), (score_mask, "score_mask"), (prob_mask_f, "prob_mask")):
                sp.dma_start(dst[:], consts[k]).then_inc(const_loaded, 16)

            def load(n, r):
                one = bass.ds(n, 1)
                for row, part in enumerate((0, 0, 1)):
                    sp.dma_start(qs[row * DH:(row + 1) * DH, r, :, :].bitcast(F32),
                                 q_src[part][one, :, :, :].rearrange("n d g t -> (n d) g t")).then_inc(stacks_loaded[r], 16)
                for row, part in enumerate(("k_hi", "k_lo", "k_hi")):
                    sp.dma_start(ks[row * DH:(row + 1) * DH, r, :].bitcast(F32),
                                 scr[part][one, :, :].rearrange("n d t -> (n d) t")).then_inc(stacks_loaded[r], 16)
                sp.dma_start(vs[:, r, :, :],
                             scr["v"][one, :, :].rearrange("n (j p) d -> p (n j) d", p=P)).then_inc(stacks_loaded[r], 16)

            def load_rows(r, half, q):
                sp.wait_ge(slot_read, q + 3)
                for row, src in enumerate((neg_hi, neg_lo)):
                    for g in range(G):
                        dst = qs[KROWS + row:KROWS + row + 1, r, g, half * HALF:(half + 1) * HALF]
                        sp.dma_start(dst.bitcast(F32), src[g * QH:(g + 1) * QH, half, :].bitcast(F32)).then_inc(rows_loaded[half], 16)

            load(0, 0)
            load(1, 1)
            load_rows(0, 0, at_a)

            def store(n, half):
                sp.wait_ge(clo_done, 2 * n + (half + 3))
                b, kv = n // NKV, n % NKV
                for buf, name in ((ctx_hi, "ctx_hi"), (ctx_lo, "ctx_lo")):
                    dst = scr[name][bass.ds(b * NQ + half * QH, QH), bass.ds(kv, 1), :, :].rearrange("t k p n -> p (t k) n")
                    sp.dma_start(dst, buf[:, half, :].bitcast(F32).rearrange("p (t n) -> p t n", n=P)).then_inc(ctx_stored[half], 16)

            def step(i, n, r, more):
                if more >= 2:
                    sp.wait_ge(unit_done, NU * n + 3)
                    load(n + 2, (r + 2) % RING)
                load_rows(r, 1, SEQ * n + (PRE + turn_position(1, more)))
                store(n, 0)
                if more:
                    load_rows((r + 1) % RING, 0, SEQ * n + (PRE + turn_position(0, more)))
                store(n, 1)
            steps(sp, step)
            for half in range(2):
                sp.wait_ge(ctx_stored[half], 32 * NG + 16)

        @block.gpsimd
        def _(pool):
            pool.memset(ones[:], 1.0).then_inc(const_ready, 1)
            pool.wait_ge(const_loaded, CONSTS)
            pool.tensor_copy(prob_mask[:], prob_mask_f[:]).then_inc(const_ready, 1)
            pool.tensor_copy(ident_b[:], ident[:]).then_inc(const_ready, 1)
            pool.sem_inc(clo_done, 2)
            with pool.Fori(0, NG, 1) as n:
                for half in range(2):
                    pool.wait_ge(ctxn_done, 2 * n + (half + 2))
                    wait_apart(pool, ctx_stored[half], 32 * n + 16, passed)
                    pool.tensor_copy(ctx_hi[:, half, :], ctxn[:, half, :]).then_inc(chi_done, 1)
                    pool.wait_ge(chi_done, 2 * n + (half + 1))
                    pool.tensor_tensor(ctx_lo[:, half, :], ctxn[:, half, :], ctx_hi[:, half, :].bitcast(F32),
                                       ALU.subtract).then_inc(clo_done, 1)

        @block.tensor
        def _(pe):
            pe.sem_inc(slot_read, 2)
            pe.sem_inc(exp_done, 2)
            pe.sem_inc(unit_done, 3)
            pe.sem_inc(recip_done, 1)
            pe.sem_inc(ctxn_done, 1)
            for half in range(2):
                pe.sem_inc(rows_loaded[half], 16)
                pe.sem_inc(ctx_stored[half], 16)
            pe.wait_ge(const_ready, 4)
            pe.wait_ge(const_loaded, CONSTS)

            def slot_item(it, r, q, parity, all_read=False):
                kind, i, g = it
                pe.wait_ge(slot_read, q + (2 if all_read else 1))
                if kind == "turn":
                    pe.transpose(ps[0:G * QH, 2 * parity, 0:P],
                                 row_max[:, i, :, :].rearrange("p g q -> p (g q)"), ident[:]).then_inc(slot_filled, 1)
                    return
                keys = (i + 1) * P
                for c in range(0, keys, HALF):
                    wide = min(HALF, keys - c)
                    last = pe.matmul(ps[:, 2 * parity + c // HALF, 0:wide], qs[0:KROWS, r, g, i * P:(i + 1) * P],
                                     ks[0:KROWS, r, c:c + wide], start=True, stop=True)
                last.then_inc(slot_filled, 1)

            def scores(n, r, u, g):
                half, j = units[u]
                a, z = queries(u)
                out = ps[:, 4 + g % 2, 0:z - a]
                if j == 0 and g == 0:
                    pe.wait_ge(rows_loaded[half], 32 * G * n + (32 * G + 16))
                pe.wait_ge(exp_done, NU * G * n + (u * G + g + 1))
                diagonal = a == j * P
                last = pe.matmul(out, ks[:, r, j * P:(j + 1) * P], qs[:, r, g, a:z], start=True, stop=not diagonal)
                if diagonal:
                    last = pe.matmul(out[:, 0:P], ident_b[:], prob_mask[:], start=False, stop=True)
                last.then_inc(scores_done, 1)

            def products(n, r, u, kind):
                half, j = units[u]
                a, z = queries(u)
                at = slice(a - half * HALF, z - half * HALF)
                if kind == "ctx":
                    pe.wait_ge(exp_done, NU * G * n + (G * (u + 1) + 2))
                if j == 0:
                    pe.wait_ge(ctxn_done if kind == "ctx" else recip_done, 2 * n + (half + 1))
                bank = ctx_ps if kind == "ctx" else sum_ps
                for g in range(G):
                    stat = vs[:, r, j, :] if kind == "ctx" else ones[:]
                    last = pe.matmul(bank[g * DH:(g + 1) * DH, at], stat, probs[:, u % 3, g, 0:z - a],
                                     start=j == 0, stop=j == QH * (half + 1) - 1)
                if kind == "sum":
                    last.then_inc(unit_done, 1)

            pe.wait_ge(stacks_loaded[0], 16 * 7)
            for q, it in enumerate(first):
                slot_item(it, 0, q, q % 2)
            for g in range(G):
                scores(0, 0, 0, g)

            def step(i, n, r, more):
                after = (r + 1) % RING
                for u in range(NU):
                    for part, kind in enumerate(("ctx", "sum")):
                        for g in (2 * part, 2 * part + 1):
                            if u + 1 < NU:
                                scores(n, r, u + 1, g)
                            elif more:
                                scores(n + 1, after, 0, g)
                        for p, it in place_items(2 * u + part, more):
                            if it == ("row", 0, 0):
                                pe.wait_ge(stacks_loaded[after], i * 112 + ((r + 1) // RING * 112 + 112))
                            slot_item(it, after, SEQ * n + (PRE + p), (PRE + p) % 2, all_read=not more)
                        products(n, r, u, kind)
            steps(pe, step)

        @block.scalar
        def _(act):
            def negative(n, half, q, parity):
                act.wait_ge(slot_filled, q + 1)
                act.wait_ge(rows_loaded[half], 32 * G * n + 16)
                act.activation(neg_hi[:, half, :], ps[0:G * QH, 2 * parity, 0:P], ACT.Copy, scale=-1.0).then_inc(neg_hi_done, 1)

            def exps(n, u, g):
                a, z = queries(u)
                if g == 0:
                    act.wait_ge(unit_done, NU * n + (u + 1))
                act.wait_ge(scores_done, NU * G * n + (u * G + g + 1))
                act.activation(probs[:, u % 3, g, 0:z - a], ps[:, 4 + g % 2, 0:z - a], ACT.Exp,
                               scale=SCALE).then_inc(exp_done, 1)

            negative(0, 0, at_a, at_a % 2)
            for g in range(G):
                exps(0, 0, g)

            def step(i, n, r, more):
                for u in range(NU):
                    for part in range(2):
                        for g in (2 * part, 2 * part + 1):
                            if u + 1 < NU:
                                exps(n, u + 1, g)
                            elif more:
                                exps(n + 1, 0, g)
                        for p, it in place_items(2 * u + part, more):
                            if it[0] == "turn":
                                negative(n if it[1] else n + 1, it[1], SEQ * n + (PRE + p), (PRE + p) % 2)
            steps(act, step)

        @block.vector
        def _(dve):
            dve.memset(ks[KROWS:KROWS + 2, :, :].bitcast(F32), 1.0).then_inc(const_ready, 1)
            dve.wait_ge(const_loaded, CONSTS)

            def slot_item(it, n, q, parity):
                kind, i, g = it
                if kind == "turn":
                    dve.wait_ge(neg_hi_done, 2 * n + (i + 1))
                    dve.scalar_tensor_tensor(neg_lo[:, i, :], ps[0:G * QH, 2 * parity, 0:P], -1.0,
                                             neg_hi[:, i, :].bitcast(F32), ALU.mult, ALU.subtract).then_inc(slot_read, 1)
                    return
                keys = (i + 1) * P
                src = ps[:, 2 * parity:2 * parity + 2, :].rearrange("p a n -> p (a n)")[:, 0:keys]
                wait_apart(dve, slot_filled, q + 1, passed)
                dve.tensor_tensor_reduce(out=src, in0=src, in1=score_mask[:, T - keys:T], scale=1.0,
                                         scalar=-3.0e38, op0=ALU.add, op1=ALU.max,
                                         accum_out=row_max[:, i // QH, g, i % QH:i % QH + 1]).then_inc(slot_read, 1)

            def end_chunk(n, half):
                dve.wait_ge(unit_done, NU * n + ((QH if half == 0 else NU) + 3))
                dve.reciprocal(recip[:], sum_ps).then_inc(recip_done, 1)
                dve.wait_ge(recip_done, 2 * n + (half + 2))
                dve.wait_ge(clo_done, 2 * n + (half + 1))
                dve.tensor_tensor(ctxn[:, half, :], ctx_ps, recip[:], ALU.mult).then_inc(ctxn_done, 1)

            for q, it in enumerate(first):
                slot_item(it, 0, q, q % 2)

            def step(i, n, r, more):
                for k in range(2 * NU):
                    for p, it in place_items(k, more):
                        slot_item(it, n if it == ("turn", 1, 0) else n + 1, SEQ * n + (PRE + p), (PRE + p) % 2)
                    if k == 2 * QH - 1:
                        end_chunk(n, 0)
                end_chunk(n, 1)
            steps(dve, step)


def build(nc, ins, consts, out):
    x = ins["L0_attn_resid"].rearrange("b t d -> (b t) d")
    y = out.rearrange("b t d -> (b t) d")
    ffn_w = {k: ins["L0_ffn_" + k] for k in ("gate_w", "base_w", "base_b", "lora_A", "lora_B")}
    attn_w = {k: ins["L0_attn_" + k] for k in ("Wq", "Wk", "Wv")}
    x1 = nc.dram_tensor("x1", (N, D), F32).ap()
    scr = {k: nc.dram_tensor(f"scr_{k}", shape, dt).ap() for k, shape, dt in (
        ("q_hi", (NG, G * DH, T), F32), ("q_lo", (NG, G * DH, T), F32),
        ("k_hi", (NG, DH, T), F32), ("k_lo", (NG, DH, T), F32), ("v", (NG, T, DH), F32),
        ("ctx_hi", (NT, NKV, P, P), F32), ("ctx_lo", (NT, NKV, P, P), F32))}
    ffn_stage(nc, "f1", x, x1, ffn_w, consts)
    qkv_stage(nc, x1, attn_w, consts, scr)
    attention_stage(nc, consts, scr)
    ffn_stage(nc, "f2", x1, y, ffn_w, consts,
              attn={"wo": ins["L0_attn_Wo"], "ctx_hi": scr["ctx_hi"], "ctx_lo": scr["ctx_lo"]})


def shape_constants():
    f = np.float32
    idx = np.arange(0, DH, 2, dtype=f) / f(DH)
    freq = f(1.0 / (2.0 * np.pi)) * np.power(f(500000.0), -idx)
    factor, lo, hi, length = 32.0, 1.0, 4.0, 2048
    scaled = np.where(freq < f(lo / length), freq / f(factor), freq)
    smooth = np.clip((f(length) * freq - f(lo)) / f(hi - lo), f(0), f(1))
    mid = (freq >= f(lo / length)) & (freq <= f(hi / length))
    freq = np.where(mid, (f(1) - smooth) * (freq / f(factor)) + smooth * freq, scaled).astype(f)
    phase = f(2.0 * np.pi) * np.arange(T, dtype=f)[None, :] * freq[:, None]
    sign = np.concatenate([-np.ones(DH // 2, f), np.ones(DH // 2, f)])[:, None]
    cos = np.tile(np.cos(phase), (2, 1)).astype(f)
    sin = (np.tile(np.sin(phase), (2, 1)) * sign).astype(f)
    above = np.triu(np.full((P, P), NEG, f), 1)
    score_mask = np.zeros((P, T), f)
    score_mask[:, T - P:] = above
    return {"identity": np.eye(P, dtype=f), "expert": np.tile(np.arange(E, dtype=f), (P, 1)),
            "rope_cos": np.tile(cos, (P // DH, 1)), "rope_sin": np.tile(sin, (P // DH, 1)),
            "score_mask": score_mask, "prob_mask": np.ascontiguousarray(above.T)}


def kernel(**inputs):
    import concourse.bacc as bacc
    from concourse.bass_utils import run_bass_kernel_spmd

    nc = bacc.Bacc("TRN2", target_bir_lowering=False, num_devices=1)
    arrays, ins, consts = {}, {}, {}
    for group, named in ((ins, inputs), (consts, shape_constants())):
        for k, a in named.items():
            a = np.ascontiguousarray(a)
            arrays["in_" + k] = a
            group[k] = nc.dram_tensor("in_" + k, a.shape, mybir.dt.from_np(a.dtype), kind="ExternalInput").ap()
    out = nc.dram_tensor("out_x", (B, T, D), F32, kind="ExternalOutput").ap()
    build(nc, ins, consts, out)
    r = run_bass_kernel_spmd(nc, [arrays], core_ids=[0])
    return r.results[0]["out_x"]
```

```python
from contextlib import ExitStack

import numpy as np

import concourse.bass as bass
from concourse import mybir

F32 = mybir.dt.float32
F32R = mybir.dt.float32r
BF16 = mybir.dt.bfloat16
U32 = mybir.dt.uint32
ALU = mybir.AluOpType
ACT = mybir.ActivationFunctionType

P = 128
B, T, D = 2, 1024, 1024
N = B * T
KC = D // P
NT = N // P
HALF = 512
NH, NKV, DH = 32, 8, 32
G = NH // NKV
NG = B * NKV
E, R = 8, 16
ER = E * R
EPS = 1e-5
ROUTE = 10
NEG = -1.0e30


def split_products(pe, out, stat_hi, stat_lo, mov_hi, mov_lo, start, stop):
    pe.matmul(out, stat_hi, mov_hi, start=start, stop=False)
    pe.matmul(out, stat_hi, mov_lo, start=False, stop=False)
    return pe.matmul(out, stat_lo, mov_hi, start=False, stop=stop)


def wait_apart(eng, sem, value, passed):
    eng.wait_ge(sem, value)
    eng.sem_inc(passed, 1)


def ffn_weights(nc, ctx, name):
    def pair(n, shape):
        return [ctx.enter_context(nc.sbuf_tensor(f"{name}_{n}_{part}", shape, F32R)) for part in ("hi", "lo")]
    return {"wt": pair("wt", [P, KC, D]),
            "ag": pair("ag", [P, KC, ER + E]),
            "bt": pair("bt", [P, D])}


def flat(tile):
    return tile[:, :, :].rearrange("p c n -> p (c n)") if len(tile.shape) == 3 else tile[:, :]


def ffn_stage(nc, name, x_src, x_dst, fw, base_b, consts, prep=None, attn=None):
    RAW = 4
    PIECE = KC * D // NT
    with ExitStack() as ctx:
        def sb(n, shape, dt):
            return ctx.enter_context(nc.sbuf_tensor(f"{name}_{n}", shape, dt))

        def sem(n):
            return ctx.enter_context(nc.semaphore(f"{name}_{n}"))

        (wt_hi, wt_lo), (ag_hi, ag_lo), (bt_hi, bt_lo) = fw["wt"], fw["ag"], fw["bt"]
        if prep:
            raw = sb("raw", [P, RAW, D], F32)
            wq_raw = sb("wq_raw", [P, 2, PIECE], F32)
            wq_hi, wq_lo = prep["wq"]
        if attn:
            wo_hi = sb("wo_hi", [P, KC, D], F32R)
            wo_lo = sb("wo_lo", [P, KC, D], F32R)
            ctxT = sb("ctxT", [P, 2, 2, KC, P], F32R)
        x_ring = sb("x_ring", [P, 4, D], F32)
        half_bias = sb("half_bias", [P, D], F32)
        h = sb("h", [P, D], F32)
        wo_raw = [x_ring[:, 2, :], x_ring[:, 3, :], h[:]]
        hT_hi = sb("hT_hi", [P, 2, KC, P], F32R)
        hT_lo = sb("hT_lo", [P, 2, KC, P], F32R)
        stats = sb("stats", [P, 2, 6], F32)
        mv = sb("mv", [P, 2], F32)
        std = sb("std", [P, 1], F32)
        rstd = sb("rstd", [P, 1], F32)
        eps = sb("eps", [P, 1], F32)
        top = sb("top", [P, 8], F32)
        top_idx = sb("top_idx", [P, 8], U32)
        idx_f = sb("idx_f", [P, 2], F32)
        gap = sb("gap", [P, 1], F32)
        expgap = sb("expgap", [P, 1], F32)
        onep = sb("onep", [P, 1], F32)
        w1 = sb("w1", [P, 1], F32)
        w2 = sb("w2", [P, 1], F32)
        wf1 = sb("wf1", [P, E], F32)
        wf2 = sb("wf2", [P, E], F32)
        w_full = sb("w_full", [P, E, 1], F32)
        low_s = sb("low_s", [P, ER], F32)
        lowT_hi = sb("lowT_hi", [P, P], F32R)
        lowT_lo = sb("lowT_lo", [P, P], F32R)
        ident = sb("ident", [P, P], F32)
        expert = sb("expert", [P, E], F32)

        ps = ctx.enter_context(nc.psum_tensor(f"{name}_ps", [P, 8, HALF], F32))
        hT_ps = ps[:, 0:2, :].rearrange("p a (c n) -> p (a c) n", n=P)
        ffn_ps = ps[:, 2:4, :]
        wo_ps = ps[:, 4:6, :]
        turn_ps = [ps[:, 2 * i:2 * i + 2, :].rearrange("p a (c n) -> p (a c) n", n=P) for i in (1, 2)]
        gl_ps = ps[:, 6, 0:ER + E]
        lowT_ps = ps[:, 7, 0:P]

        items = ([("gate", 0), ("A", 0), ("B", 0)] + [("base", o) for o in range(KC)]) if prep else []
        EARLY = 2

        def raw_count(i):
            return 16 * sum(1 for j in range(i + 1) if j % RAW == i % RAW and items[j][0] != "B")

        x_loaded = [sem(f"x_loaded{s}") for s in range(4)]
        if prep:
            raw_loaded = [sem(f"raw_loaded{s}") for s in range(RAW)]
            b_loaded = sem("b_loaded")
            raw_turned = sem("raw_turned")
            copy_stored = sem("copy_stored")
            wq_loaded = [sem(f"wq_loaded{s}") for s in range(2)]
            wq_hi_done = sem("wq_hi_done")
            wq_lo_done = sem("wq_lo_done")
        if attn:
            wo_loaded = [sem(f"wo_loaded{s}") for s in range(len(wo_raw))]
            ctx_loaded = [sem(f"ctx_loaded{s}") for s in range(2)]
            wo_done = sem("wo_done")
            wo_added = sem("wo_added")
        passed = sem("passed")
        const_loaded = sem("const_loaded")
        CONSTS = 2 * 16
        eps_set = sem("eps_set")
        bias_loaded = sem("bias_loaded")
        w_hi_done = sem("w_hi_done")
        w_lo_done = sem("w_lo_done")
        ln_step = sem("ln_step")
        std_ready = sem("std_ready")
        h_ready = sem("h_ready")
        h_turned = sem("h_turned")
        hT_hi_done = sem("hT_hi_done")
        hT_lo_done = sem("hT_lo_done")
        gl_done = sem("gl_done")
        route = sem("route")
        exp_done = sem("exp_done")
        low_ready = sem("low_ready")
        low_turned = sem("low_turned")
        lowT_hi_done = sem("lowT_hi_done")
        lowT_lo_done = sem("lowT_lo_done")
        ffn_done = sem("ffn_done")
        ffn_added = sem("ffn_added")
        bias_ready = sem("bias_ready")
        bias_added = sem("bias_added")
        stored = [sem(f"stored{s}") for s in range(4)]

        def x_wait(eng, i, u):
            eng.wait_ge(x_loaded[u % 4], (i + u // 4) * 16 + 16)

        def load_x(eng, t, s):
            eng.dma_start(x_ring[:, s, :], x_src[bass.ds(t * P, P), :]).then_inc(x_loaded[s], 16)

        def load_ctx(eng, t, par):
            for part, src in enumerate((attn["ctx_hi"], attn["ctx_lo"])):
                eng.dma_start(ctxT[:, par, part, :, :].bitcast(F32), src[bass.ds(t, 1), :, :, :].rearrange("t c p n -> p (t c) n")).then_inc(ctx_loaded[par], 16)

        def run_tiles(eng, step):
            with eng.Fori(0, NT // 4 - 1, 1) as i:
                for u in range(4):
                    step(i, 4 * i + u, u, 3)
            for u in range(4):
                step(NT // 4 - 1, NT - 4 + u, u, 3 - u)

        def turned_view(n, kind):
            v = turn_ps[n % 2]
            return v[:, :, 0:E] if kind == "gate" else v

        def weight_view(kind, k, part):
            if kind == "base":
                return (wt_hi, wt_lo)[part][:, :, k * P:(k + 1) * P]
            if kind == "A":
                return (ag_hi, ag_lo)[part][:, :, 0:ER]
            if kind == "gate":
                return (ag_hi, ag_lo)[part][:, :, ER:ER + E]
            if kind == "B":
                return (bt_hi, bt_lo)[part][:, :].rearrange("p (c n) -> p c n", n=P)
            assert False

        def wq_piece(part, i, u):
            return flat((wq_hi, wq_lo)[part])[:, bass.ds((4 * i + u) * PIECE, PIECE)]

        block = ctx.enter_context(nc.Block())

        @block.sync
        def _(sp):
            sp.dma_start(ident[:], consts["identity"]).then_inc(const_loaded, 16)
            sp.dma_start(expert[:], consts["expert"]).then_inc(const_loaded, 16)
            if attn:
                load_ctx(sp, 0, 0)
                load_ctx(sp, 1, 1)
                for k in range(KC):
                    if k >= len(wo_raw):
                        sp.wait_ge(w_lo_done, k - len(wo_raw) + 1)
                    sp.dma_start(wo_raw[k % len(wo_raw)], attn["wo"][k * P:(k + 1) * P, :]).then_inc(wo_loaded[k % len(wo_raw)], 16)
            load_x(sp, 0, 0)
            for i, (kind, k) in enumerate(items):
                s = i % RAW
                if i >= RAW:
                    sp.wait_ge(raw_turned, i - RAW + 1)
                if kind == "B":
                    with nc.allow_non_contiguous_dma("64-byte runs of lora_B"):
                        for e in range(E):
                            dst = raw[:, s, :].rearrange("p (c e r) -> p c e r", e=E, r=R)[:, :, e, :]
                            ins = sp.dma_start(dst, prep["lora_B"][e].rearrange("(c p) r -> p c r", p=P))
                            ins.then_inc(b_loaded, 16)
                elif kind == "gate":
                    sp.dma_start(raw[0:E, s, :], prep["gate_w"]).then_inc(raw_loaded[s], 16)
                elif kind == "A":
                    sp.dma_start(raw[:, s, :], prep["lora_A"].rearrange("e r d -> (e r) d")).then_inc(raw_loaded[s], 16)
                else:
                    sp.dma_start(raw[:, s, :], prep["base_w"][k * P:(k + 1) * P, :]).then_inc(raw_loaded[s], 16)
            load_x(sp, 1, 1)
            sp.dma_start(half_bias[:], base_b.rearrange("(a n) -> a n", a=1).broadcast_to([P, D])).then_inc(bias_loaded, 16)
            if attn:
                sp.wait_ge(w_lo_done, KC)
            load_x(sp, 2, 2)
            if prep:
                sp.wait_ge(w_lo_done, len(items))
                for key in ("ag", "bt"):
                    for part in range(2):
                        sp.dma_start(prep["copy"][key][part], flat(fw[key][part]).bitcast(F32)).then_inc(copy_stored, 16)

            def step(i, t, u, more):
                if attn and more >= 2:
                    sp.wait_ge(wo_done, 2 * t + 2)
                    load_ctx(sp, t + 2, u % 2)
                if more >= 3:
                    s = (u + 3) % 4
                    sp.wait_ge(stored[s], (i + (u + 3) // 4) * 16 + (16 if s == 3 else 0))
                    load_x(sp, t + 3, s)
                if prep:
                    piece = bass.ds((4 * i + u) * PIECE, PIECE)
                    sp.wait_ge(wq_lo_done, 4 * i + (u + 1))
                    sp.dma_start(wq_raw[:, u % 2, :], prep["Wq"][bass.ds((2 * i + u // 2) * P, P), (u % 2) * PIECE:(u % 2 + 1) * PIECE]).then_inc(wq_loaded[u % 2], 16)
                    for part in range(2):
                        sp.dma_start(prep["copy"]["wt"][part][:, piece], flat(fw["wt"][part])[:, piece].bitcast(F32)).then_inc(copy_stored, 16)
                sp.wait_ge(ffn_added, 2 * t + 4)
                sp.dma_start(x_dst[bass.ds(t * P, P), :], x_ring[:, u, :]).then_inc(stored[u], 16)
            run_tiles(sp, step)
            for s in range(4):
                sp.wait_ge(stored[s], 16 * (NT // 4) + (16 if s == 3 else 0))
            if prep:
                sp.wait_ge(copy_stored, 16 * (4 + 2 * NT))

        @block.gpsimd
        def _(pool):
            pool.memset(eps[:], EPS).then_inc(eps_set, 1)
            pool.sem_inc(stored[3], 16)
            pool.wait_ge(bias_loaded, 16)
            pool.tensor_scalar(half_bias[:], half_bias[:], 0.5, None, ALU.mult).then_inc(bias_ready, 1)
            pool.wait_ge(bias_ready, 1)
            with pool.Fori(0, NT // 4, 1) as i:
                for u in range(4):
                    pool.wait_ge(h_ready, 4 * i + u + 1)
                    pool.tensor_tensor(x_ring[:, u, :], x_ring[:, u, :], half_bias[:], ALU.add).then_inc(bias_added, 1)
                    if prep:
                        pool.wait_ge(wq_hi_done, 4 * i + (u + 1))
                        pool.tensor_tensor(wq_piece(1, i, u), wq_raw[:, u % 2, :], wq_piece(0, i, u).bitcast(F32),
                                           ALU.subtract).then_inc(wq_lo_done, 1)

        @block.tensor
        def _(pe):
            pe.sem_inc(ffn_added, 2)
            pe.sem_inc(low_turned, 1)
            pe.sem_inc(ffn_done, 1)
            if attn:
                pe.sem_inc(wo_added, 2)
            if prep:
                pe.sem_inc(wq_lo_done, 2)
            pe.wait_ge(const_loaded, CONSTS)

            def turn_raw(i):
                kind, s = items[i][0], i % RAW
                if kind == "B":
                    pe.wait_ge(b_loaded, 16 * E)
                else:
                    pe.wait_ge(raw_loaded[s], raw_count(i))
                if i >= 2:
                    pe.wait_ge(w_lo_done, i - 1)
                out = turn_ps[i % 2]
                for c in range(KC):
                    if kind == "gate":
                        last = pe.transpose(out[:, c, 0:E], raw[0:E, s, c * P:(c + 1) * P], ident[0:E, 0:E])
                    else:
                        last = pe.transpose(out[:, c, :], raw[:, s, c * P:(c + 1) * P], ident[:])
                last.then_inc(raw_turned, 1)

            def turn_h(t):
                pe.wait_ge(h_ready, t + 1)
                pe.wait_ge(hT_lo_done, t)
                for c in range(KC):
                    last = pe.transpose(hT_ps[:, c, :], h[:, c * P:(c + 1) * P], ident[:])
                last.then_inc(h_turned, 1)

            def low_and_gate(t, par):
                pe.wait_ge(hT_lo_done, t + 1)
                pe.wait_ge(low_ready, t)
                for c in range(KC):
                    last = split_products(pe, gl_ps, hT_hi[:, par, c, :], hT_lo[:, par, c, :],
                                          ag_hi[:, c, :], ag_lo[:, c, :], c == 0, c == KC - 1)
                last.then_inc(gl_done, 1)

            def base(t, par, half):
                pe.wait_ge(ffn_added, 2 * t + half + 1)
                cols = slice(half * HALF, (half + 1) * HALF)
                for c in range(KC):
                    split_products(pe, ffn_ps[:, half, :], hT_hi[:, par, c, :], hT_lo[:, par, c, :],
                                   wt_hi[:, c, cols], wt_lo[:, c, cols], c == 0, False)

            def turn_low(t):
                pe.wait_ge(low_ready, t + 1)
                pe.transpose(lowT_ps, low_s[:], ident[:]).then_inc(low_turned, 1)

            def lora(t):
                pe.wait_ge(lowT_lo_done, t + 1)
                for half in range(2):
                    cols = slice(half * HALF, (half + 1) * HALF)
                    split_products(pe, ffn_ps[:, half, :], lowT_hi[:], lowT_lo[:], bt_hi[:, cols], bt_lo[:, cols],
                                   False, True).then_inc(ffn_done, 1)

            def project(t, u):
                par = u % 2
                pe.wait_ge(ctx_loaded[par], 32 * (t // 2) + 32)
                for half in range(2):
                    pe.wait_ge(wo_added, 2 * t + half + 1)
                    cols = slice(half * HALF, (half + 1) * HALF)
                    for c in range(KC):
                        last = split_products(pe, wo_ps[:, half, :], ctxT[:, par, 0, c, :], ctxT[:, par, 1, c, :],
                                              wo_hi[:, c, cols], wo_lo[:, c, cols], c == 0, c == KC - 1)
                    last.then_inc(wo_done, 1)

            if attn:
                pe.wait_ge(ctx_loaded[0], 32)
                pe.wait_ge(ctx_loaded[1], 32)
                for c in range(KC):
                    pe.wait_ge(w_lo_done, c + 1)
                    for t, banks in enumerate((wo_ps, ffn_ps)):
                        for half in range(2):
                            cols = slice(half * HALF, (half + 1) * HALF)
                            last = split_products(pe, banks[:, half, :], ctxT[:, t, 0, c, :], ctxT[:, t, 1, c, :],
                                                  wo_hi[:, c, cols], wo_lo[:, c, cols], c == 0, c == KC - 1)
                            if c == KC - 1:
                                last.then_inc(wo_done, 1)
            if prep:
                for i in range(EARLY):
                    turn_raw(i)
            turn_h(0)
            if prep:
                pe.wait_ge(w_lo_done, EARLY)
            low_and_gate(0, 0)
            for i in range(EARLY, len(items)):
                turn_raw(i)
            if prep:
                pe.wait_ge(w_lo_done, len(items))
            if attn:
                pe.wait_ge(wo_added, 2 + 4)

            def step(i, t, u, more):
                if more >= 1:
                    turn_h(t + 1)
                base(t, u % 2, 0)
                turn_low(t)
                if attn and more >= 2:
                    project(t + 2, u + 2)
                base(t, u % 2, 1)
                lora(t)
                if more >= 1:
                    low_and_gate(t + 1, (u + 1) % 2)
            run_tiles(pe, step)

        @block.scalar
        def _(act):
            def high_weight(i):
                kind, k = items[i]
                act.wait_ge(raw_turned, i + 1)
                act.activation(weight_view(kind, k, 0), turned_view(i, kind), ACT.Copy,
                               scale=0.5 if kind == "base" else 1.0).then_inc(w_hi_done, 1)

            def high_hT(t, par):
                act.wait_ge(h_turned, t + 1)
                act.activation(hT_hi[:, par, :, :], hT_ps, ACT.Copy).then_inc(hT_hi_done, 1)

            def deviation(t):
                act.wait_ge(ln_step, 4 * t + 3)
                act.activation(std[:], mv[:, 1:2], ACT.Sqrt, bias=eps[:, 0:1]).then_inc(std_ready, 1)

            act.wait_ge(eps_set, 1)
            if attn:
                for k in range(KC):
                    act.wait_ge(wo_loaded[k % len(wo_raw)], 16 * (k // len(wo_raw) + 1))
                    act.activation(wo_hi[:, k, :], wo_raw[k % len(wo_raw)], ACT.Copy).then_inc(w_hi_done, 1)
            if prep:
                for i in range(EARLY):
                    high_weight(i)
            deviation(0)
            high_hT(0, 0)
            for i in range(EARLY, len(items)):
                high_weight(i)
            deviation(1)

            def step(i, t, u, more):
                act.wait_ge(route, ROUTE * t + 3)
                act.activation(expgap[:], gap[:], ACT.Exp).then_inc(exp_done, 1)
                act.wait_ge(ffn_done, 2 * t + 1)
                if more >= 1:
                    high_hT(t + 1, (u + 1) % 2)
                act.wait_ge(low_turned, t + 2)
                act.activation(lowT_hi[:], lowT_ps, ACT.Copy).then_inc(lowT_hi_done, 1)
                if more >= 2:
                    deviation(t + 2)
                if prep:
                    act.wait_ge(wq_loaded[u % 2], (2 * i + u // 2) * 16 + 16)
                    act.activation(wq_piece(0, i, u), wq_raw[:, u % 2, :], ACT.Copy).then_inc(wq_hi_done, 1)
            run_tiles(act, step)

        @block.vector
        def _(dve):
            def low_weight(i):
                kind, k = items[i]
                src = turned_view(i, kind)
                dve.wait_ge(w_hi_done, i + 1)
                if kind == "base":
                    for c in range(0, KC, 4):
                        last = dve.scalar_tensor_tensor(weight_view(kind, k, 1)[:, c:c + 4, :], src[:, c:c + 4, :], 0.5,
                                                 weight_view(kind, k, 0)[:, c:c + 4, :].bitcast(F32), ALU.mult, ALU.subtract)
                    last.then_inc(w_lo_done, 1)
                else:
                    dve.tensor_tensor(weight_view(kind, k, 1), src, weight_view(kind, k, 0).bitcast(F32),
                                      ALU.subtract).then_inc(w_lo_done, 1)

            def layer_norm(i, t, u):
                x = x_ring[:, u % 4, :]
                if attn is None:
                    x_wait(dve, i, u)
                else:
                    dve.wait_ge(wo_added, 2 * t + 4)
                for half in range(2):
                    dve.bn_stats(stats[:, half, :], x[:, half * HALF:(half + 1) * HALF]).then_inc(ln_step, 1)
                wait_apart(dve, ln_step, 4 * t + 2, passed)
                dve.bn_aggr(mv[:], stats[:, :, :].rearrange("p a b -> p (a b)")).then_inc(ln_step, 1)
                dve.wait_ge(std_ready, t + 1)
                dve.reciprocal(rstd[:], std[:]).then_inc(ln_step, 1)
                dve.wait_ge(ln_step, 4 * t + 4)
                dve.wait_ge(h_turned, t)
                dve.tensor_scalar(h[:], x, mv[:, 0:1], rstd[:, 0:1], ALU.subtract, ALU.mult).then_inc(h_ready, 1)

            def low_hT(t, par):
                dve.wait_ge(hT_hi_done, t + 1)
                dve.tensor_tensor(hT_lo[:, par, :, :], hT_ps, hT_hi[:, par, :, :].bitcast(F32),
                                  ALU.subtract).then_inc(hT_lo_done, 1)

            def routing(t):
                logits = gl_ps[:, ER:ER + E]
                wait_apart(dve, gl_done, t + 1, passed)
                dve.max(top[:], logits).then_inc(route, 1)
                wait_apart(dve, route, ROUTE * t + 1, passed)
                dve.max_index(top_idx[:], top[:], logits).then_inc(route, 1)
                dve.tensor_tensor(gap[:], top[:, 1:2], top[:, 0:1], ALU.subtract).then_inc(route, 1)
                dve.wait_ge(route, ROUTE * t + 3)
                dve.tensor_copy(idx_f[:], top_idx[:, 0:2]).then_inc(route, 1)
                dve.wait_ge(exp_done, t + 1)
                dve.tensor_scalar(onep[:], expgap[:], 1.0, None, ALU.add).then_inc(route, 1)
                dve.wait_ge(route, ROUTE * t + 5)
                dve.reciprocal(w1[:], onep[:]).then_inc(route, 1)
                dve.wait_ge(route, ROUTE * t + 6)
                dve.tensor_tensor(w2[:], expgap[:], w1[:], ALU.mult).then_inc(route, 1)
                dve.tensor_scalar(wf1[:], expert[:], idx_f[:, 0:1], w1[:, 0:1], ALU.is_equal, ALU.mult).then_inc(route, 1)
                dve.wait_ge(route, ROUTE * t + 8)
                dve.tensor_scalar(wf2[:], expert[:], idx_f[:, 1:2], w2[:, 0:1], ALU.is_equal, ALU.mult).then_inc(route, 1)
                dve.wait_ge(route, ROUTE * t + 9)
                dve.tensor_tensor(w_full[:, :, 0], wf1[:], wf2[:], ALU.add).then_inc(route, 1)
                dve.wait_ge(route, ROUTE * t + 10)
                dve.wait_ge(low_turned, t + 1)
                dve.tensor_tensor(low_s[:].rearrange("p (e r) -> p e r", r=R),
                                  gl_ps[:, 0:ER].rearrange("p (e r) -> p e r", r=R),
                                  w_full[:].broadcast_to([P, E, R]), ALU.mult).then_inc(low_ready, 1)

            def add_projection(i, t, u, banks=wo_ps):
                x_wait(dve, i, u)
                for half in range(2):
                    cols = slice(half * HALF, (half + 1) * HALF)
                    dve.wait_ge(wo_done, 2 * t + half + 1)
                    dve.tensor_tensor(x_ring[:, u % 4, cols], banks[:, half, :], x_ring[:, u % 4, cols],
                                      ALU.add).then_inc(wo_added, 1)

            dve.wait_ge(const_loaded, CONSTS)
            if attn:
                for k in range(KC):
                    dve.wait_ge(w_hi_done, k + 1)
                    dve.tensor_tensor(wo_lo[:, k, :], wo_raw[k % len(wo_raw)], wo_hi[:, k, :].bitcast(F32),
                                      ALU.subtract).then_inc(w_lo_done, 1)
                dve.wait_ge(w_lo_done, KC)
                add_projection(0, 0, 0)
            if prep:
                for i in range(EARLY):
                    low_weight(i)
            layer_norm(0, 0, 0)
            if attn:
                add_projection(0, 1, 1, ffn_ps)
            low_hT(0, 0)
            for i in range(EARLY, len(items)):
                low_weight(i)
            layer_norm(0, 1, 1)

            def step(i, t, u, more):
                routing(t)
                if more >= 1:
                    low_hT(t + 1, (u + 1) % 2)
                dve.wait_ge(lowT_hi_done, t + 1)
                dve.tensor_tensor(lowT_lo[:], lowT_ps, lowT_hi[:].bitcast(F32), ALU.subtract).then_inc(lowT_lo_done, 1)
                if more >= 2:
                    if attn:
                        add_projection(i, t + 2, u + 2)
                    layer_norm(i, t + 2, u + 2)
                dve.wait_ge(bias_added, t + 1)
                for half in range(2):
                    cols = slice(half * HALF, (half + 1) * HALF)
                    dve.wait_ge(ffn_done, 2 * t + (half + 2))
                    dve.tensor_tensor(x_ring[:, u, cols], ffn_ps[:, half, :], x_ring[:, u, cols],
                                      ALU.add).then_inc(ffn_added, 1)
            run_tiles(dve, step)


def qkv_stage(nc, x_src, wq, w, consts, scr):
    NCH = T // HALF
    TC = HALF // P
    KV = NKV * DH
    WRAW = 4
    NO = KC + KV // P
    with ExitStack() as ctx:
        def sb(n, shape, dt):
            return ctx.enter_context(nc.sbuf_tensor(f"qkv_{n}", shape, dt))

        def sem(n):
            return ctx.enter_context(nc.semaphore(f"qkv_{n}"))

        wq_hi, wq_lo = wq
        wkv_hi = sb("wkv_hi", [P, KC, 2 * KV], F32R)
        wkv_lo = sb("wkv_lo", [P, KC, 2 * KV], F32R)
        wkv_raw = sb("wkv_raw", [P, WRAW, 2 * KV], F32)
        hT_hi = sb("hT_hi", [P, NCH, KC, HALF], F32R)
        hT_lo = sb("hT_lo", [P, NCH, KC, HALF], F32R)
        x_ring = sb("x_ring", [P, 2, D], F32)
        h = sb("h", [P, D], F32)
        stats = sb("stats", [P, 2, 6], F32)
        mv = sb("mv", [P, 2], F32)
        std = sb("std", [P, 1], F32)
        rstd = sb("rstd", [P, 1], F32)
        eps = sb("eps", [P, 1], F32)
        cos = sb("cos", [P, T], F32)
        sin = sb("sin", [P, T], F32)
        rot = sb("rot", [P, 2, HALF], F32)
        rope = sb("rope", [P, 2, HALF], F32)
        rope_hi = sb("rope_hi", [P, 2, HALF], F32R)
        rope_lo = sb("rope_lo", [P, 2, HALF], F32R)
        v_out = sb("v_out", [P, 2, KV], F32)
        ident = sb("ident", [P, P], F32)

        ps = ctx.enter_context(nc.psum_tensor("qkv_ps", [P, 8, HALF], F32))
        hT_ps = ps[:, 0:2, :].rearrange("p a (c n) -> p (a c) n", n=P)

        wkv_loaded = [sem(f"wkv_loaded{s}") for s in range(WRAW)]
        x_loaded = [sem(f"x_loaded{s}") for s in range(2)]
        passed = sem("passed")
        const_loaded = sem("const_loaded")
        CONSTS = 3 * 16
        eps_set = sem("eps_set")
        wkv_hi_done = sem("wkv_hi_done")
        wkv_lo_done = sem("wkv_lo_done")
        ln_step = sem("ln_step")
        std_ready = sem("std_ready")
        h_ready = sem("h_ready")
        h_turned = sem("h_turned")
        hT_hi_done = sem("hT_hi_done")
        hT_lo_done = sem("hT_lo_done")
        proj_done = sem("proj_done")
        cos_done = sem("cos_done")
        swapped = sem("swapped")
        sin_done = sem("sin_done")
        rope_done = sem("rope_done")
        hi_done = sem("hi_done")
        lo_done = sem("lo_done")
        out_stored = [sem(f"out_stored{s}") for s in range(2)]
        v_done = sem("v_done")
        v_copied = sem("v_copied")
        v_stored = [sem(f"v_stored{s}") for s in range(2)]

        k_rows = scr["k_hi"].rearrange("n r t -> (n r) t"), scr["k_lo"].rearrange("n r t -> (n r) t")

        block = ctx.enter_context(nc.Block())

        def run_chunks(eng, step):
            with eng.Fori(0, B - 1, 1) as b:
                for ch in range(NCH):
                    step(b, ch, True)
            for ch in range(NCH):
                step(B - 1, ch, ch + 1 < NCH)

        @block.sync
        def _(sp):
            sp.dma_start(ident[:], consts["identity"]).then_inc(const_loaded, 16)

            def load_x(t, slot):
                sp.wait_ge(h_ready, t + 1)
                sp.dma_start(x_ring[:, slot, :], x_src[bass.ds(t * P, P), :]).then_inc(x_loaded[slot], 16)

            for t in range(TC):
                load_x(t, t % 2)
            sp.dma_start(cos[:], consts["rope_cos"]).then_inc(const_loaded, 16)
            sp.dma_start(sin[:], consts["rope_sin"]).then_inc(const_loaded, 16)
            for j in range(KC):
                if j >= WRAW:
                    sp.wait_ge(wkv_lo_done, j - WRAW + 1)
                for cols, src in ((slice(0, KV), w["Wk"]), (slice(KV, 2 * KV), w["Wv"])):
                    sp.dma_start(wkv_raw[:, j % WRAW, cols], src[j * P:(j + 1) * P, :]).then_inc(wkv_loaded[j % WRAW], 16)
            with sp.Fori(TC // 2, NT // 2, 1) as i:
                for slot in range(2):
                    load_x(2 * i + slot, slot)

        @block.tensor
        def _(pe):
            pe.sem_inc(h_ready, 2)
            pe.sem_inc(cos_done, 4)
            pe.sem_inc(rope_done, 2)
            pe.sem_inc(lo_done, 2)
            pe.sem_inc(v_copied, 2)
            for first_free in (hT_lo_done, h_turned, v_done):
                pe.sem_inc(first_free, 1)
            for first_free in out_stored + v_stored:
                pe.sem_inc(first_free, 16)
            pe.wait_ge(const_loaded, 16)

            def turn_h(b, t):
                tile = b * (NCH * TC) + t
                pe.wait_ge(h_ready, tile + 3)
                pe.wait_ge(hT_lo_done, tile + 1)
                for c in range(KC):
                    last = pe.transpose(hT_ps[:, c, :], h[:, c * P:(c + 1) * P], ident[:])
                last.then_inc(h_turned, 1)

            for t in range(TC):
                turn_h(0, t)

            def step(b, ch, more):
                pe.wait_ge(hT_lo_done, b * (NCH * TC) + ((ch + 1) * TC + 1))
                for o in range(NO):
                    g = ch * NO + o
                    if o == KC:
                        pe.wait_ge(wkv_lo_done, KC)
                    pe.wait_ge(cos_done, b * (NCH * NO) + (g + 1))
                    wh, wl = (wq_hi, wq_lo) if o < KC else (wkv_hi, wkv_lo)
                    cols = slice((o % KC) * P, (o % KC + 1) * P)
                    for c in range(KC):
                        last = split_products(pe, ps[:, 2 + g % 4, :], wh[:, c, cols], wl[:, c, cols],
                                              hT_hi[:, ch, c, :], hT_lo[:, ch, c, :], c == 0, c == KC - 1)
                    last.then_inc(proj_done, 1)
                    if more and o % 2 == 1 and o // 2 < TC:
                        turn_h(b, (ch + 1) * TC + o // 2)
                for s in range(TC):
                    t = ch * TC + s
                    pe.wait_ge(v_copied, b * (NCH * TC) + (t + 1))
                    for c in range(KC):
                        tok = slice(s * P, (s + 1) * P)
                        last = split_products(pe, ps[:, 6 + t % 2, 0:KV], hT_hi[:, ch, c, tok], hT_lo[:, ch, c, tok],
                                              wkv_hi[:, c, KV:2 * KV], wkv_lo[:, c, KV:2 * KV], c == 0, c == KC - 1)
                    last.then_inc(v_done, 1)
            run_chunks(pe, step)

        @block.scalar
        def _(act):
            def deviation(b, t):
                act.wait_ge(ln_step, b * (4 * NCH * TC) + (4 * t + 3))
                act.activation(std[:], mv[:, 1:2], ACT.Sqrt, bias=eps[:, 0:1]).then_inc(std_ready, 1)

            def high_hT(b, t):
                tile = b * (NCH * TC) + t
                act.wait_ge(h_turned, tile + 2)
                act.activation(hT_hi[:, (t // TC) % NCH, :, (t % TC) * P:(t % TC + 1) * P], hT_ps, ACT.Copy).then_inc(hT_hi_done, 1)

            def high_out(b, g):
                act.wait_ge(rope_done, b * (NCH * NO) + (g + 3))
                act.wait_ge(out_stored[g % 2], b * (NCH * NO * 16) + (g // 2) * 32 + 16)
                act.activation(rope_hi[:, g % 2, :], rope[:, g % 2, :], ACT.Copy).then_inc(hi_done, 1)

            def store_out(b, g):
                ch, o = g // NO, g % NO
                cols = slice(ch * HALF, (ch + 1) * HALF)
                act.wait_ge(hi_done, b * (NCH * NO) + (g + 1))
                act.wait_ge(lo_done, b * (NCH * NO) + (g + 3))
                for part, buf in enumerate((rope_hi, rope_lo)):
                    q_group = scr[("q_hi", "q_lo")[part]][bass.ds(b * NKV + o % KC, 1), ch, :, :]
                    rows = q_group.rearrange("n r t -> (n r) t") if o < KC \
                        else k_rows[part][bass.ds(b * KV + (o - KC) * P, P), cols]
                    act.dma_start(rows, buf[:, g % 2, :].bitcast(F32)).then_inc(out_stored[g % 2], 16)

            def store_v(b, t):
                act.wait_ge(v_copied, b * (NCH * TC) + (t + 3))
                dst = scr["v"][bass.ds(b * NKV, NKV), t * P:(t + 1) * P, :].rearrange("n t d -> t n d")
                act.dma_start(dst, v_out[:, t % 2, :].rearrange("p (n d) -> p n d", d=DH)).then_inc(v_stored[t % 2], 16)

            act.wait_ge(eps_set, 1)
            for t in range(TC):
                deviation(0, t)
                high_hT(0, t)
            for j in range(KC):
                act.wait_ge(wkv_loaded[j % WRAW], 32 * (j // WRAW + 1))
                act.activation(wkv_hi[:, j, :], wkv_raw[:, j % WRAW, :], ACT.Copy).then_inc(wkv_hi_done, 1)

            def step(b, ch, more):
                act.wait_ge(v_done, b * (NCH * TC) + (ch * TC + 1))
                for o in range(NO):
                    g = ch * NO + o
                    if more and o % 2 == 0 and o // 2 < TC:
                        deviation(b, (ch + 1) * TC + o // 2)
                    if o >= 1:
                        high_out(b, g - 1)
                    if o >= 2:
                        store_out(b, g - 2)
                    if more and o % 2 == 1 and o // 2 < TC:
                        high_hT(b, (ch + 1) * TC + o // 2)
                high_out(b, ch * NO + NO - 1)
                store_out(b, ch * NO + NO - 2)
                store_out(b, ch * NO + NO - 1)
                for s in range(TC):
                    t = ch * TC + s
                    act.wait_ge(v_done, b * (NCH * TC) + (t + 2))
                    act.wait_ge(v_stored[t % 2], b * (NCH * TC * 8) + (t // 2) * 16 + 16)
                    act.activation(v_out[:, t % 2, :], ps[:, 6 + t % 2, 0:KV], ACT.Copy).then_inc(v_copied, 1)
                    store_v(b, t)
            run_chunks(act, step)
            for s in range(2):
                act.wait_ge(out_stored[s], B * NCH * NO * 16 + 16)
                act.wait_ge(v_stored[s], B * NCH * TC * 8 + 16)

        @block.gpsimd
        def _(pool):
            pool.memset(eps[:], EPS).then_inc(eps_set, 1)
            for j in range(KC):
                pool.wait_ge(wkv_hi_done, j + 1)
                pool.tensor_tensor(wkv_lo[:, j, :], wkv_raw[:, j % WRAW, :], wkv_hi[:, j, :].bitcast(F32),
                                   ALU.subtract).then_inc(wkv_lo_done, 1)
            pool.wait_ge(const_loaded, CONSTS)

            def low_part(b, g):
                pool.wait_ge(hi_done, b * (NCH * NO) + (g + 1))
                pool.tensor_tensor(rope_lo[:, g % 2, :], rope[:, g % 2, :], rope_hi[:, g % 2, :].bitcast(F32),
                                   ALU.subtract).then_inc(lo_done, 1)

            with pool.Fori(0, B, 1) as b:
                for g in range(NCH * NO):
                    cols = slice((g // NO) * HALF, (g // NO + 1) * HALF)
                    pool.wait_ge(swapped, b * (NCH * NO) + (g + 1))
                    pool.tensor_tensor(rot[:, g % 2, :], rot[:, g % 2, :], sin[:, cols], ALU.mult).then_inc(sin_done, 1)
                    if g % NO >= 1:
                        low_part(b, g - 1)
                    if g % NO == NO - 1:
                        low_part(b, g)

        @block.vector
        def _(dve):
            def layer_norm(b, t):
                tile = b * (NCH * TC) + t
                x = x_ring[:, t % 2, :]
                dve.wait_ge(x_loaded[t % 2], b * (NCH * TC * 8) + 16 * (t // 2 + 1))
                for half in range(2):
                    dve.bn_stats(stats[:, half, :], x[:, half * HALF:(half + 1) * HALF]).then_inc(ln_step, 1)
                wait_apart(dve, ln_step, 4 * tile + 2, passed)
                dve.bn_aggr(mv[:], stats[:, :, :].rearrange("p a b -> p (a b)")).then_inc(ln_step, 1)
                dve.wait_ge(std_ready, tile + 1)
                dve.reciprocal(rstd[:], std[:]).then_inc(ln_step, 1)
                dve.wait_ge(ln_step, 4 * tile + 4)
                dve.wait_ge(h_turned, tile + 1)
                dve.tensor_scalar(h[:], x, mv[:, 0:1], rstd[:, 0:1], ALU.subtract, ALU.mult).then_inc(h_ready, 1)

            def low_hT(b, t):
                at = (slice(None), (t // TC) % NCH, slice(None), slice((t % TC) * P, (t % TC + 1) * P))
                dve.wait_ge(hT_hi_done, b * (NCH * TC) + (t + 1))
                dve.tensor_tensor(hT_lo[at], hT_ps, hT_hi[at].bitcast(F32), ALU.subtract).then_inc(hT_lo_done, 1)

            def rope_sum(b, g):
                dve.wait_ge(sin_done, b * (NCH * NO) + (g + 1))
                dve.wait_ge(cos_done, b * (NCH * NO) + (g + 5))
                dve.tensor_tensor(rope[:, g % 2, :], rope[:, g % 2, :], rot[:, g % 2, :], ALU.add).then_inc(rope_done, 1)

            swap = [(i + DH // 2) % DH for i in range(DH)]
            for t in range(TC):
                layer_norm(0, t)
                low_hT(0, t)
            dve.wait_ge(const_loaded, CONSTS)

            def step(b, ch, more):
                cols = slice(ch * HALF, (ch + 1) * HALF)
                for o in range(NO):
                    g = ch * NO + o
                    bank = ps[:, 2 + g % 4, :]
                    if more and o % 2 == 0 and o // 2 < TC:
                        layer_norm(b, (ch + 1) * TC + o // 2)
                    dve.wait_ge(proj_done, b * (NCH * NO) + (g + 1))
                    wait_apart(dve, rope_done, b * (NCH * NO) + (g + 1), passed)
                    dve.stream_shuffle(rot[:, g % 2, :], bank, swap).then_inc(swapped, 1)
                    dve.wait_ge(lo_done, b * (NCH * NO) + (g + 1))
                    dve.tensor_tensor(rope[:, g % 2, :], bank, cos[:, cols], ALU.mult).then_inc(cos_done, 1)
                    if o >= 1:
                        rope_sum(b, g - 1)
                    if more and o % 2 == 1 and o // 2 < TC:
                        low_hT(b, (ch + 1) * TC + o // 2)
                rope_sum(b, ch * NO + NO - 1)
            run_chunks(dve, step)


def attention_stage(nc, consts, scr, fw, copy):
    NQ = T // P
    QH = NQ // 2
    RING = 3
    SLOTS = 3
    BANKS = 3
    PROBS = 4
    AHEAD = 2
    PIECES = 4
    KROWS = 3 * DH
    LOADS = 7 * 16
    PIECE = KC * D // NG
    ROW_LOADS = 2 * 16
    SCALE = float(DH) ** -0.5
    with ExitStack() as ctx:
        def sb(n, shape, dt):
            return ctx.enter_context(nc.sbuf_tensor(f"at_{n}", shape, dt))

        def sem(n):
            return ctx.enter_context(nc.semaphore(f"at_{n}"))

        qs = sb("qs", [KROWS + 2, RING, 2, G, HALF], F32R)
        ks = sb("ks", [KROWS + 2, RING, T], F32R)
        vs = sb("vs", [P, RING, NQ, DH], F32)
        ones = sb("ones", [P, DH], F32)
        probs = sb("probs", [P, PROBS, G, HALF], F32)
        row_max = sb("row_max", [P, 2, G, QH], F32)
        part_max = sb("part_max", [P, G, QH], F32)
        neg_hi = sb("neg_hi", [G * QH, 2, P], F32R)
        neg_lo = sb("neg_lo", [G * QH, 2, P], F32R)
        score_mask = sb("score_mask", [P, T], F32)
        ident = sb("ident", [P, P], F32)
        sums = sb("sums", [P, HALF], F32)
        recip = sb("recip", [P, HALF], F32)
        ctxn = sb("ctxn", [P, 2, HALF], F32)
        ctx_hi = sb("ctx_hi", [P, 2, HALF], F32R)
        ctx_lo = sb("ctx_lo", [P, 2, HALF], F32R)

        ps = ctx.enter_context(nc.psum_tensor("at_ps", [P, 8, HALF], F32))
        slot_ps = [ps[:, b, :] for b in range(SLOTS)]
        score_ps = [ps[:, SLOTS + b, :] for b in range(BANKS)]
        ctx_ps = ps[:, 6, :]
        sum_ps = ps[:, 7, :]

        stacks_loaded = [sem(f"stacks_loaded{r}") for r in range(RING)]
        passed = sem("passed")
        const_loaded = sem("const_loaded")
        const_ready = sem("const_ready")
        fw_loaded = sem("fw_loaded")
        slot_filled = sem("slot_filled")
        slot_read = sem("slot_read")
        neg_hi_done = sem("neg_hi_done")
        rows_loaded = [sem(f"rows_loaded{h}") for h in range(2)]
        scores_done = sem("scores_done")
        exp_done = sem("exp_done")
        mask_done = sem("mask_done")
        unit_done = sem("unit_done")
        sum_copied = sem("sum_copied")
        ctx_copied = sem("ctx_copied")
        recip_done = sem("recip_done")
        mult_done = sem("mult_done")
        chi_done = sem("chi_done")
        clo_done = sem("clo_done")
        ctx_stored = [sem(f"ctx_stored{h}") for h in range(2)]

        units = [(half, j) for half in range(2) for j in range(QH * (half + 1))]
        NU = len(units)
        LAST = {QH - 1: 0, NU - 1: 1}

        def queries(u):
            half, j = units[u]
            return max(half * HALF, j * P), (half + 1) * HALF

        diagonal = [u for u in range(NU) if queries(u)[0] == units[u][1] * P]

        rows = [("row", i, g, c) for i in range(NQ) for c in range(i // QH + 1) for g in range(G)]
        at_a = QH * G + G
        first = rows[:at_a] + [("turn", 0)] + rows[at_a:]
        TURN_B = ("turn", 1)

        def row_keys(i, c):
            return min(HALF, (i + 1) * P - c * HALF)

        weight = [row_keys(it[1], it[3]) + 60 if it[0] == "row" else 150 for it in first]
        room = [queries(u)[1] - queries(u)[0] + 150 for u in range(NU)]
        places = [[] for _ in range(NU)]
        done, at = 0.0, 0
        for it, wgt in zip(first, weight):
            while at < NU - 1 and sum(room[:at + 1]) / sum(room) < (done + wgt / 2) / sum(weight):
                at += 1
            places[at].append(it)
            done += wgt
        assert len(places[0]) >= SLOTS
        places[0].insert(SLOTS - 1, TURN_B)
        SEQ = len(first) + 1
        PRE = len(first)

        def place_items(u, more):
            if not more:
                return [(0, TURN_B)] if u == 0 else []
            start = sum(len(pl) for pl in places[:u])
            return [(start + x, it) for x, it in enumerate(places[u])]

        def position(item, more):
            return next(p for u in range(NU) for p, it in place_items(u, more) if it == item)

        def ahead(n, nm, u, more):
            if u + AHEAD < NU:
                return n, nm, u + AHEAD
            return (n + 1, (nm + 1) % RING, u + AHEAD - NU) if more else None

        q_src = [scr[k].rearrange("n h (g d) t -> n d (h g) t", d=DH) for k in ("q_hi", "q_lo")]

        def first_step_over(n):
            return not isinstance(n, int) or n > 0

        block = ctx.enter_context(nc.Block())

        def steps(eng, step):
            step(0, 0, 0, 2)
            loops = (NG - 2) // RING
            with eng.Fori(0, loops, 1) as i:
                for r in range(RING):
                    step(RING * i + (r + 1), (r + 1) % RING, i + (r + 2) // RING, 2 if NG - 1 - RING * loops >= 2 else 1)
            for n in range(RING * loops + 1, NG):
                step(n, n % RING, (n + 1) // RING, min(NG - 1 - n, 2))

        @block.sync
        def _(sp):
            for dst, k in ((ident, "identity"), (score_mask, "score_mask")):
                sp.dma_start(dst[:], consts[k]).then_inc(const_loaded, 16)

            def load(n, nm):
                one = bass.ds(n, 1)
                for row, part in enumerate((0, 0, 1)):
                    sp.dma_start(qs[row * DH:(row + 1) * DH, nm, :, :, :].rearrange("p h g t -> p (h g) t").bitcast(F32),
                                 q_src[part][one, :, :, :].rearrange("n d g t -> (n d) g t")).then_inc(stacks_loaded[nm], 16)
                for row, part in enumerate(("k_hi", "k_lo", "k_hi")):
                    sp.dma_start(ks[row * DH:(row + 1) * DH, nm, :].bitcast(F32),
                                 scr[part][one, :, :].rearrange("n d t -> (n d) t")).then_inc(stacks_loaded[nm], 16)
                sp.dma_start(vs[:, nm, :, :],
                             scr["v"][one, :, :].rearrange("n (j p) d -> p (n j) d", p=P)).then_inc(stacks_loaded[nm], 16)

            def load_rows(nm, half, q):
                sp.wait_ge(slot_read, q + (SLOTS + 1))
                for row, src in enumerate((neg_hi, neg_lo)):
                    dst = qs[KROWS + row:KROWS + row + 1, nm, half, :, :].rearrange("p g t -> p (g t)")
                    sp.dma_start(dst.bitcast(F32), src[:, half, :].bitcast(F32)).then_inc(rows_loaded[half], 16)

            def store(n, half):
                sp.wait_ge(clo_done, 2 * n + (half + 3))
                b, kv = n // NKV, n % NKV
                for buf, name in ((ctx_hi, "ctx_hi"), (ctx_lo, "ctx_lo")):
                    dst = scr[name][bass.ds(b * NQ + half * QH, QH), bass.ds(kv, 1), :, :].rearrange("t k p n -> p (t k) n")
                    sp.dma_start(dst, buf[:, half, :].bitcast(F32).rearrange("p (t n) -> p t n", n=P)).then_inc(ctx_stored[half], 16)

            load(0, 0)
            load(1, 1)
            load_rows(0, 0, at_a)
            for key in ("ag", "bt"):
                for part in range(2):
                    sp.dma_start(flat(fw[key][part]).bitcast(F32), copy[key][part]).then_inc(fw_loaded, 16)

            def step(n, nm, _, more):
                load_rows(nm, 1, SEQ * n + (PRE + position(TURN_B, more)))
                if more >= 2:
                    sp.wait_ge(unit_done, NU * n + PROBS)
                    load(n + 2, (nm + 2) % RING)
                for part in range(2):
                    sp.dma_start(flat(fw["wt"][part])[:, bass.ds(n * PIECE, PIECE)].bitcast(F32),
                                 copy["wt"][part][:, bass.ds(n * PIECE, PIECE)]).then_inc(fw_loaded, 16)
                if more:
                    load_rows((nm + 1) % RING, 0, SEQ * n + (PRE + position(("turn", 0), more)))
                if first_step_over(n):
                    store(n - 1, 1)
                store(n, 0)
            steps(sp, step)
            store(NG - 1, 1)
            for half in range(2):
                sp.wait_ge(ctx_stored[half], 32 * NG + 16)
            sp.wait_ge(fw_loaded, 16 * (4 + 2 * NG))

        @block.gpsimd
        def _(pool):
            pool.memset(ones[:], 1.0).then_inc(const_ready, 1)
            pool.sem_inc(clo_done, 2)

            def mask(n, u):
                tile = probs[:, u % PROBS, :, 0:P]
                wait_apart(pool, exp_done, NU * G * n + (G * (u + 1) + BANKS), passed)
                pool.affine_select(out=tile, in_=tile, compare_op=ALU.is_ge, fill=0.0, base=0,
                                   pattern=[[0, G], [1, P]], channel_multiplier=-1).then_inc(mask_done, 1)

            def divide(n, half):
                pool.wait_ge(recip_done, 2 * PIECES * n + (PIECES * (half + 1) + 1))
                pool.wait_ge(ctx_copied, 2 * n + (half + 2))
                pool.tensor_tensor(ctxn[:, half, :], ctxn[:, half, :], recip[:], ALU.mult).then_inc(mult_done, 1)

            def low(n, half):
                pool.wait_ge(chi_done, 2 * n + (half + 1))
                pool.tensor_tensor(ctx_lo[:, half, :], ctxn[:, half, :], ctx_hi[:, half, :].bitcast(F32),
                                   ALU.subtract).then_inc(clo_done, 1)

            for u in range(AHEAD):
                mask(0, u)

            def step(n, nm, _, more):
                for u in range(NU):
                    a = ahead(n, nm, u, more)
                    if a and a[2] in diagonal:
                        mask(a[0], a[2])
                    if first_step_over(n) and u == 4:
                        divide(n - 1, 1)
                    if first_step_over(n) and u == 6:
                        low(n - 1, 1)
                    if u == 9:
                        divide(n, 0)
                    if u == 11:
                        low(n, 0)
            steps(pool, step)
            divide(NG - 1, 1)
            low(NG - 1, 1)

        @block.tensor
        def _(pe):
            for count, start in ((slot_read, SLOTS), (exp_done, BANKS), (unit_done, PROBS), (sum_copied, 1),
                                 (ctx_copied, 1), (recip_done, 1), (mult_done, 1), (rows_loaded[0], 16),
                                 (rows_loaded[1], 16), (ctx_stored[0], 16), (ctx_stored[1], 16)):
                pe.sem_inc(count, start)
            pe.wait_ge(const_ready, 2)
            pe.wait_ge(const_loaded, 32)

            def slot_item(it, nm, q, slot, all_read=False):
                pe.wait_ge(slot_read, q + (SLOTS if all_read else 1))
                out = slot_ps[slot]
                if it[0] == "turn":
                    pe.transpose(out[0:G * QH, 0:P], row_max[:, it[1], :, :].rearrange("p g q -> p (g q)"),
                                 ident[:]).then_inc(slot_filled, 1)
                    return
                _, i, g, c = it
                keys = row_keys(i, c)
                pe.matmul(out[:, 0:keys], qs[0:KROWS, nm, i // QH, g, (i % QH) * P:(i % QH + 1) * P],
                          ks[0:KROWS, nm, c * HALF:c * HALF + keys], start=True, stop=True).then_inc(slot_filled, 1)

            def scores(n, nm, u, g):
                half, j = units[u]
                a, z = queries(u)
                if j == 0 and g == 0:
                    pe.wait_ge(rows_loaded[half], ROW_LOADS * n + (ROW_LOADS + 16))
                pe.wait_ge(exp_done, NU * G * n + (u * G + g + 1))
                pe.matmul(score_ps[(u * G + g) % BANKS][:, 0:z - a], ks[:, nm, j * P:(j + 1) * P], qs[:, nm, half, g, a - half * HALF:z - half * HALF],
                          start=True, stop=True).then_inc(scores_done, 1)

            def products(n, nm, u):
                half, j = units[u]
                a, z = queries(u)
                at = slice(a - half * HALF, z - half * HALF)
                if u in diagonal:
                    pe.wait_ge(mask_done, len(diagonal) * n + (diagonal.index(u) + 1))
                else:
                    pe.wait_ge(exp_done, NU * G * n + (G * (u + 1) + BANKS))
                for bank, stat, copied in ((ctx_ps, vs[:, nm, j, :], ctx_copied), (sum_ps, ones[:], sum_copied)):
                    if j == 0:
                        pe.wait_ge(copied, 2 * n + (half + 1))
                    for g in range(G):
                        last = pe.matmul(bank[g * DH:(g + 1) * DH, at], stat, probs[:, u % PROBS, g, 0:z - a],
                                         start=j == 0, stop=u in LAST)
                last.then_inc(unit_done, 1)

            pe.wait_ge(stacks_loaded[0], LOADS)
            for q, it in enumerate(first):
                slot_item(it, 0, q, q % SLOTS)
            for u in range(AHEAD):
                for g in range(G):
                    scores(0, 0, u, g)

            def step(n, nm, turns, more):
                for u in range(NU):
                    items = place_items(u, more)
                    a = ahead(n, nm, u, more)
                    cut = [0, len(items) // 4, len(items) // 2, 3 * len(items) // 4, len(items)]
                    for g in range(G):
                        if a:
                            scores(*a, g)
                        for p, it in items[cut[g]:cut[g + 1]]:
                            if it == first[0]:
                                pe.wait_ge(stacks_loaded[(nm + 1) % RING], turns * LOADS + LOADS)
                            slot_item(it, (nm + 1) % RING, SEQ * n + (PRE + p), (PRE + SEQ * nm + p) % SLOTS, not more)
                    products(n, nm, u)
            steps(pe, step)

        @block.scalar
        def _(act):
            def negative(n, half, q, slot):
                act.wait_ge(slot_filled, q + 1)
                act.wait_ge(rows_loaded[half], ROW_LOADS * n + 16)
                act.activation(neg_hi[:, half, :], slot_ps[slot][0:G * QH, 0:P], ACT.Copy, scale=-1.0).then_inc(neg_hi_done, 1)

            def exps(n, u, g):
                a, z = queries(u)
                if g == 0:
                    act.wait_ge(unit_done, NU * n + (u + 1))
                act.wait_ge(scores_done, NU * G * n + (u * G + g + 1))
                act.activation(probs[:, u % PROBS, g, 0:z - a], score_ps[(u * G + g) % BANKS][:, 0:z - a], ACT.Exp,
                               scale=SCALE).then_inc(exp_done, 1)

            def copy_chunk(n, half):
                act.wait_ge(unit_done, NU * n + (PROBS + (QH, NU)[half]))
                act.wait_ge(clo_done, 2 * n + (half + 1))
                act.activation(ctxn[:, half, :], ctx_ps, ACT.Copy).then_inc(ctx_copied, 1)
                act.wait_ge(recip_done, 2 * PIECES * n + (PIECES * half + 1))
                act.activation(sums[:], sum_ps, ACT.Copy).then_inc(sum_copied, 1)

            def high(n, half):
                act.wait_ge(mult_done, 2 * n + (half + 2))
                act.wait_ge(ctx_stored[half], 32 * n + 16)
                act.activation(ctx_hi[:, half, :], ctxn[:, half, :], ACT.Copy).then_inc(chi_done, 1)

            negative(0, 0, at_a, at_a % SLOTS)
            for u in range(AHEAD):
                for g in range(G):
                    exps(0, u, g)

            def step(n, nm, _, more):
                for u in range(NU):
                    items = place_items(u, more)
                    a = ahead(n, nm, u, more)
                    cut = [0, len(items) // 4, len(items) // 2, 3 * len(items) // 4, len(items)]
                    for g in range(G):
                        if a:
                            exps(a[0], a[2], g)
                        for p, it in items[cut[g]:cut[g + 1]]:
                            if it[0] == "turn":
                                negative(n if it[1] else n + 1, it[1], SEQ * n + (PRE + p), (PRE + SEQ * nm + p) % SLOTS)
                    if u in LAST:
                        copy_chunk(n, LAST[u])
                    if first_step_over(n) and u == 5:
                        high(n - 1, 1)
                    if u == 10:
                        high(n, 0)
            steps(act, step)
            high(NG - 1, 1)

        @block.vector
        def _(dve):
            dve.memset(ks[KROWS:KROWS + 2, :, :].bitcast(F32), 1.0).then_inc(const_ready, 1)
            dve.wait_ge(const_loaded, 32)

            def slot_item(it, n, q, slot):
                if it[0] == "turn":
                    dve.wait_ge(neg_hi_done, 2 * n + (it[1] + 1))
                    dve.scalar_tensor_tensor(neg_lo[:, it[1], :], slot_ps[slot][0:G * QH, 0:P], -1.0,
                                             neg_hi[:, it[1], :].bitcast(F32), ALU.mult, ALU.subtract).then_inc(slot_read, 1)
                    return
                _, i, g, c = it
                keys = row_keys(i, c)
                src = slot_ps[slot][:, 0:keys]
                half, tile = i // QH, i % QH
                own = slice(tile, tile + 1)
                whole = c == half
                mask = score_mask[:, T - keys:T] if whole else score_mask[:, 0:keys]
                out = row_max[:, half, g, own] if whole else part_max[:, g, own]
                if c:
                    dve.wait_ge(slot_read, q + (SLOTS - G + 1))
                wait_apart(dve, slot_filled, q + 1, passed)
                dve.tensor_tensor_reduce(out=src, in0=src, in1=mask, scale=1.0, scalar=part_max[:, g, own] if c else -3.0e38,
                                         op0=ALU.add, op1=ALU.max, accum_out=out).then_inc(slot_read, 1)

            def reciprocal(n, half, piece):
                cols = slice(piece * (HALF // PIECES), (piece + 1) * (HALF // PIECES))
                if piece == 0:
                    dve.wait_ge(sum_copied, 2 * n + (half + 2))
                    dve.wait_ge(mult_done, 2 * n + (half + 1))
                dve.reciprocal(recip[:, cols], sums[:, cols]).then_inc(recip_done, 1)

            for q, it in enumerate(first):
                slot_item(it, 0, q, q % SLOTS)

            def step(n, nm, _, more):
                for u in range(NU):
                    for p, it in place_items(u, more):
                        slot_item(it, n if it == TURN_B else n + 1, SEQ * n + (PRE + p), (PRE + SEQ * nm + p) % SLOTS)
                    if first_step_over(n) and u < PIECES:
                        reciprocal(n - 1, 1, u)
                    if 5 <= u < 5 + PIECES:
                        reciprocal(n, 0, u - 5)
            steps(dve, step)
            for piece in range(PIECES):
                reciprocal(NG - 1, 1, piece)


def build(nc, ins, consts, out):
    x = ins["L0_attn_resid"].rearrange("b t d -> (b t) d")
    y = out.rearrange("b t d -> (b t) d")
    raw = {k: ins["L0_ffn_" + k] for k in ("gate_w", "base_w", "lora_A", "lora_B")}
    base_b = ins["L0_ffn_base_b"]
    attn_w = {k: ins["L0_attn_" + k] for k in ("Wk", "Wv")}
    x1 = nc.dram_tensor("x1", (N, D), F32).ap()
    scr = {k: nc.dram_tensor(f"scr_{k}", shape, dt).ap() for k, shape, dt in (
        ("q_hi", (NG, T // HALF, G * DH, HALF), F32), ("q_lo", (NG, T // HALF, G * DH, HALF), F32),
        ("k_hi", (NG, DH, T), F32), ("k_lo", (NG, DH, T), F32), ("v", (NG, T, DH), F32),
        ("ctx_hi", (NT, NKV, P, P), F32), ("ctx_lo", (NT, NKV, P, P), F32))}
    copy = {k: [nc.dram_tensor(f"copy_{k}_{part}", (P, n), F32).ap() for part in ("hi", "lo")]
            for k, n in (("wt", KC * D), ("ag", KC * (ER + E)), ("bt", D))}
    with ExitStack() as ctx:
        wq = [ctx.enter_context(nc.sbuf_tensor(f"wq_{part}", [P, KC, D], F32R)) for part in ("hi", "lo")]
        with ExitStack() as inner:
            fw = ffn_weights(nc, inner, "f1")
            ffn_stage(nc, "f1", x, x1, fw, base_b, consts, prep={"wq": wq, "Wq": ins["L0_attn_Wq"], "copy": copy, **raw})
        qkv_stage(nc, x1, wq, attn_w, consts, scr)
    with ExitStack() as ctx:
        fw = ffn_weights(nc, ctx, "f2")
        attention_stage(nc, consts, scr, fw, copy)
        ffn_stage(nc, "f2", x1, y, fw, base_b, consts,
                  attn={"wo": ins["L0_attn_Wo"], "ctx_hi": scr["ctx_hi"], "ctx_lo": scr["ctx_lo"]})


def shape_constants():
    f = np.float32
    idx = np.arange(0, DH, 2, dtype=f) / f(DH)
    freq = f(1.0 / (2.0 * np.pi)) * np.power(f(500000.0), -idx)
    factor, lo, hi, length = 32.0, 1.0, 4.0, 2048
    scaled = np.where(freq < f(lo / length), freq / f(factor), freq)
    smooth = np.clip((f(length) * freq - f(lo)) / f(hi - lo), f(0), f(1))
    mid = (freq >= f(lo / length)) & (freq <= f(hi / length))
    freq = np.where(mid, (f(1) - smooth) * (freq / f(factor)) + smooth * freq, scaled).astype(f)
    phase = f(2.0 * np.pi) * np.arange(T, dtype=f)[None, :] * freq[:, None]
    sign = np.concatenate([-np.ones(DH // 2, f), np.ones(DH // 2, f)])[:, None]
    cos = np.tile(np.cos(phase), (2, 1)).astype(f)
    sin = (np.tile(np.sin(phase), (2, 1)) * sign).astype(f)
    above = np.triu(np.full((P, P), NEG, f), 1)
    score_mask = np.zeros((P, T), f)
    score_mask[:, T - P:] = above
    return {"identity": np.eye(P, dtype=f), "expert": np.tile(np.arange(E, dtype=f), (P, 1)),
            "rope_cos": np.tile(cos, (P // DH, 1)), "rope_sin": np.tile(sin, (P // DH, 1)),
            "score_mask": score_mask}


def kernel(**inputs):
    import concourse.bacc as bacc
    from concourse.bass_utils import run_bass_kernel_spmd

    nc = bacc.Bacc("TRN2", target_bir_lowering=False, num_devices=1)
    arrays, ins, consts = {}, {}, {}
    for group, named in ((ins, inputs), (consts, shape_constants())):
        for k, a in named.items():
            a = np.ascontiguousarray(a)
            arrays["in_" + k] = a
            group[k] = nc.dram_tensor("in_" + k, a.shape, mybir.dt.from_np(a.dtype), kind="ExternalInput").ap()
    out = nc.dram_tensor("out_x", (B, T, D), F32, kind="ExternalOutput").ap()
    build(nc, ins, consts, out)
    r = run_bass_kernel_spmd(nc, [arrays], core_ids=[0])
    return r.results[0]["out_x"]
```

```python
from contextlib import ExitStack

import numpy as np

import concourse.bass as bass
from concourse import mybir

F32 = mybir.dt.float32
F32R = mybir.dt.float32r
BF16 = mybir.dt.bfloat16
U32 = mybir.dt.uint32
ALU = mybir.AluOpType
ACT = mybir.ActivationFunctionType

P = 128
B, T, D = 2, 1024, 1024
N = B * T
KC = D // P
NT = N // P
HALF = 512
NH, NKV, DH = 32, 8, 32
G = NH // NKV
NG = B * NKV
E, R = 8, 16
ER = E * R
WIDE = D + ER + E
EPS = 1e-5
ROUTE = 10
NEG = -1.0e30


def split_products(pe, out, stat_hi, stat_lo, mov_hi, mov_lo, start, stop):
    pe.matmul(out, stat_hi, mov_hi, start=start, stop=False)
    pe.matmul(out, stat_hi, mov_lo, start=False, stop=False)
    return pe.matmul(out, stat_lo, mov_hi, start=False, stop=stop)


def wait_apart(eng, sem, value, passed):
    eng.wait_ge(sem, value)
    eng.sem_inc(passed, 1)


def ffn_weights(nc, ctx, name):
    def pair(n, shape):
        return [ctx.enter_context(nc.sbuf_tensor(f"{name}_{n}_{part}", shape, F32R)) for part in ("hi", "lo")]
    return {"wt": pair("wt", [P, KC, WIDE]),
            "bt": pair("bt", [P, D])}


def flat(tile):
    return tile[:, :, :].rearrange("p c n -> p (c n)") if len(tile.shape) == 3 else tile[:, :]


def ffn_stage(nc, name, x_src, x_dst, fw, base_b, consts, prep=None, attn=None):
    RAW = 4
    PIECE = KC * D // NT
    COPY = KC * WIDE // NT
    with ExitStack() as ctx:
        def sb(n, shape, dt):
            return ctx.enter_context(nc.sbuf_tensor(f"{name}_{n}", shape, dt))

        def sem(n):
            return ctx.enter_context(nc.semaphore(f"{name}_{n}"))

        (wt_hi, wt_lo), (bt_hi, bt_lo) = fw["wt"], fw["bt"]
        if prep:
            raw = sb("raw", [P, RAW, D], F32)
            wq_raw = sb("wq_raw", [P, 2, PIECE], F32)
            wq_hi, wq_lo = prep["wq"]
        if attn:
            wo_hi = sb("wo_hi", [P, KC, D], F32R)
            wo_lo = sb("wo_lo", [P, KC, D], F32R)
            ctxT = sb("ctxT", [P, 2, 2, KC, P], F32R)
        x_ring = sb("x_ring", [P, 4, D], F32)
        half_bias = sb("half_bias", [P, D], F32)
        h = sb("h", [P, D], F32)
        wo_raw = [x_ring[:, 2, :], x_ring[:, 3, :], h[:]]
        hT_hi = sb("hT_hi", [P, 2, KC, P], F32R)
        hT_lo = sb("hT_lo", [P, 2, KC, P], F32R)
        stats = sb("stats", [P, 2, 6], F32)
        mv = sb("mv", [P, 2], F32)
        std = sb("std", [P, 1], F32)
        rstd = sb("rstd", [P, 1], F32)
        eps = sb("eps", [P, 1], F32)
        top = sb("top", [P, 8], F32)
        top_idx = sb("top_idx", [P, 8], U32)
        idx_f = sb("idx_f", [P, 2], F32)
        gap = sb("gap", [P, 1], F32)
        expgap = sb("expgap", [P, 1], F32)
        onep = sb("onep", [P, 1], F32)
        w1 = sb("w1", [P, 1], F32)
        w2 = sb("w2", [P, 1], F32)
        wf1 = sb("wf1", [P, E], F32)
        wf2 = sb("wf2", [P, E], F32)
        w_full = sb("w_full", [P, E, 1], F32)
        low_s = sb("low_s", [P, ER], F32)
        lowT_hi = sb("lowT_hi", [P, P], F32R)
        lowT_lo = sb("lowT_lo", [P, P], F32R)
        ident = sb("ident", [P, P], F32)
        expert = sb("expert", [P, E], F32)

        ps = ctx.enter_context(nc.psum_tensor(f"{name}_ps", [P, 8, HALF], F32))
        hT_ps = ps[:, 0:2, :].rearrange("p a (c n) -> p (a c) n", n=P)
        PARTS = [slice(0, 400), slice(400, 800), slice(800, D)]

        def part_ps(part, par):
            return ps[:, 2 + part + (par if part == 2 else 0), 0:PARTS[part].stop - PARTS[part].start]

        def gl_ps(par, a, z):
            at = D - PARTS[2].start
            return ps[:, 4 + par, at + a:at + z]

        first_ps = ps[:, 2:4, :]
        wo_ps = ps[:, 6:8, :]
        lowT_ps = ps[:, 0, 0:P]
        last_lora_ps = ps[:, 1, 0:D - PARTS[2].start]
        turn_ps = [ps[:, 2 * i:2 * i + 2, :].rearrange("p a (c n) -> p (a c) n", n=P) for i in (1, 3)]

        items = ([("gate", 0), ("A", 0)] + [("base", o) for o in range(KC)] + [("B", 0)]) if prep else []
        EARLY = 2
        TURN_H = 4
        NEXT = 10

        def raw_count(i):
            return 16 * sum(1 for j in range(i + 1) if j % RAW == i % RAW and items[j][0] != "B")

        x_loaded = [sem(f"x_loaded{s}") for s in range(4)]
        if prep:
            raw_loaded = [sem(f"raw_loaded{s}") for s in range(RAW)]
            b_loaded = sem("b_loaded")
            raw_turned = sem("raw_turned")
            copy_stored = sem("copy_stored")
            wq_loaded = [sem(f"wq_loaded{s}") for s in range(2)]
            wq_hi_done = sem("wq_hi_done")
            wq_lo_done = sem("wq_lo_done")
        if attn:
            wo_loaded = [sem(f"wo_loaded{s}") for s in range(len(wo_raw))]
            ctx_loaded = [sem(f"ctx_loaded{s}") for s in range(2)]
            wo_done = sem("wo_done")
            wo_added = sem("wo_added")
        passed = sem("passed")
        const_loaded = sem("const_loaded")
        CONSTS = 2 * 16
        eps_set = sem("eps_set")
        bias_loaded = sem("bias_loaded")
        w_hi_done = sem("w_hi_done")
        w_lo_done = sem("w_lo_done")
        ln_step = sem("ln_step")
        std_ready = sem("std_ready")
        h_ready = sem("h_ready")
        h_turned = sem("h_turned")
        hT_hi_done = sem("hT_hi_done")
        hT_lo_done = sem("hT_lo_done")
        gl_done = sem("gl_done")
        route = sem("route")
        exp_done = sem("exp_done")
        low_ready = sem("low_ready")
        low_turned = sem("low_turned")
        lowT_hi_done = sem("lowT_hi_done")
        lowT_lo_done = sem("lowT_lo_done")
        ffn_done = sem("ffn_done")
        ffn_added = sem("ffn_added")
        last_added = sem("last_added")
        bias_ready = sem("bias_ready")
        bias_added = sem("bias_added")
        stored = [sem(f"stored{s}") for s in range(4)]

        def x_wait(eng, i, u):
            eng.wait_ge(x_loaded[u % 4], (i + u // 4) * 16 + 16)

        def load_x(eng, t, s):
            eng.dma_start(x_ring[:, s, :], x_src[bass.ds(t * P, P), :]).then_inc(x_loaded[s], 16)

        def load_bias(eng):
            eng.dma_start(half_bias[:], base_b.rearrange("(a n) -> a n", a=1).broadcast_to([P, D])).then_inc(bias_loaded, 16)

        def load_ctx(eng, t, par):
            for part, src in enumerate((attn["ctx_hi"], attn["ctx_lo"])):
                eng.dma_start(ctxT[:, par, part, :, :].bitcast(F32), src[bass.ds(t, 1), :, :, :].rearrange("t c p n -> p (t c) n")).then_inc(ctx_loaded[par], 16)

        def run_tiles(eng, step):
            with eng.Fori(0, NT // 4 - 1, 1) as i:
                for u in range(4):
                    step(i, 4 * i + u, u, 3)
            for u in range(4):
                step(NT // 4 - 1, NT - 4 + u, u, 3 - u)

        def turned_view(n, kind):
            v = turn_ps[n % 2]
            return v[:, :, 0:E] if kind == "gate" else v

        def weight_view(kind, k, part):
            if kind == "base":
                return (wt_hi, wt_lo)[part][:, :, k * P:(k + 1) * P]
            if kind == "A":
                return (wt_hi, wt_lo)[part][:, :, D:D + ER]
            if kind == "gate":
                return (wt_hi, wt_lo)[part][:, :, D + ER:WIDE]
            return (bt_hi, bt_lo)[part][:, :].rearrange("p (c n) -> p c n", n=P)

        def wq_piece(part, i, u):
            return flat((wq_hi, wq_lo)[part])[:, bass.ds((4 * i + u) * PIECE, PIECE)]

        block = ctx.enter_context(nc.Block())

        @block.sync
        def _(sp):
            sp.dma_start(ident[:], consts["identity"]).then_inc(const_loaded, 16)
            sp.dma_start(expert[:], consts["expert"]).then_inc(const_loaded, 16)
            if attn:
                for k in range(KC):
                    if k == 1:
                        load_ctx(sp, 0, 0)
                    if k >= len(wo_raw):
                        sp.wait_ge(w_lo_done, k - len(wo_raw) + 1)
                    sp.dma_start(wo_raw[k % len(wo_raw)], attn["wo"][k * P:(k + 1) * P, :]).then_inc(wo_loaded[k % len(wo_raw)], 16)
                load_ctx(sp, 1, 1)
            load_x(sp, 0, 0)
            for i, (kind, k) in enumerate(items):
                s = i % RAW
                if i == NEXT - 1:
                    load_x(sp, 1, 1)
                    load_bias(sp)
                if i >= RAW:
                    sp.wait_ge(raw_turned, i - RAW + 1)
                if kind == "B":
                    with nc.allow_non_contiguous_dma("64-byte runs of lora_B"):
                        for e in range(E):
                            dst = raw[:, s, :].rearrange("p (c e r) -> p c e r", e=E, r=R)[:, :, e, :]
                            ins = sp.dma_start(dst, prep["lora_B"][e].rearrange("(c p) r -> p c r", p=P))
                            ins.then_inc(b_loaded, 16)
                elif kind == "gate":
                    sp.dma_start(raw[0:E, s, :], prep["gate_w"]).then_inc(raw_loaded[s], 16)
                elif kind == "A":
                    sp.dma_start(raw[:, s, :], prep["lora_A"].rearrange("e r d -> (e r) d")).then_inc(raw_loaded[s], 16)
                else:
                    sp.dma_start(raw[:, s, :], prep["base_w"][k * P:(k + 1) * P, :]).then_inc(raw_loaded[s], 16)
            if attn:
                load_x(sp, 1, 1)
                load_bias(sp)
            if attn:
                sp.wait_ge(w_lo_done, KC)
            load_x(sp, 2, 2)
            if prep:
                sp.wait_ge(w_lo_done, len(items))
                for part in range(2):
                    sp.dma_start(prep["copy"]["bt"][part], flat(fw["bt"][part]).bitcast(F32)).then_inc(copy_stored, 16)

            def step(i, t, u, more):
                if attn and more >= 2:
                    sp.wait_ge(wo_done, 2 * t + 2)
                    load_ctx(sp, t + 2, u % 2)
                if more >= 3:
                    s = (u + 3) % 4
                    sp.wait_ge(stored[s], (i + (u + 3) // 4) * 16 + (16 if s == 3 else 0))
                    load_x(sp, t + 3, s)
                if prep:
                    piece = bass.ds((4 * i + u) * COPY, COPY)
                    sp.wait_ge(wq_lo_done, 4 * i + (u + 1))
                    sp.dma_start(wq_raw[:, u % 2, :], prep["Wq"][bass.ds((2 * i + u // 2) * P, P), (u % 2) * PIECE:(u % 2 + 1) * PIECE]).then_inc(wq_loaded[u % 2], 16)
                    for part in range(2):
                        sp.dma_start(prep["copy"]["wt"][part][:, piece], flat(fw["wt"][part])[:, piece].bitcast(F32)).then_inc(copy_stored, 16)
                sp.wait_ge(ffn_added, 3 * t + 6)
                sp.dma_start(x_dst[bass.ds(t * P, P), :], x_ring[:, u, :]).then_inc(stored[u], 16)
            run_tiles(sp, step)
            for s in range(4):
                sp.wait_ge(stored[s], 16 * (NT // 4) + (16 if s == 3 else 0))
            if prep:
                sp.wait_ge(copy_stored, 16 * (2 + 2 * NT))

        @block.gpsimd
        def _(pool):
            pool.memset(eps[:], EPS).then_inc(eps_set, 1)
            pool.sem_inc(stored[3], 16)
            pool.wait_ge(bias_loaded, 16)
            pool.tensor_scalar(half_bias[:], half_bias[:], 0.5, None, ALU.mult).then_inc(bias_ready, 1)
            pool.wait_ge(bias_ready, 1)
            with pool.Fori(0, NT // 4, 1) as i:
                for u in range(4):
                    pool.wait_ge(h_ready, 4 * i + u + 1)
                    pool.tensor_tensor(x_ring[:, u, :], x_ring[:, u, :], half_bias[:], ALU.add).then_inc(bias_added, 1)
                    if prep:
                        pool.wait_ge(wq_hi_done, 4 * i + (u + 1))
                        pool.tensor_tensor(wq_piece(1, i, u), wq_raw[:, u % 2, :], wq_piece(0, i, u).bitcast(F32),
                                           ALU.subtract).then_inc(wq_lo_done, 1)

        @block.tensor
        def _(pe):
            pe.sem_inc(ffn_added, 3)
            pe.sem_inc(low_turned, 1)
            pe.sem_inc(lowT_lo_done, 1)
            pe.sem_inc(ffn_done, 1)
            if attn:
                pe.sem_inc(wo_added, 2)
            if prep:
                pe.sem_inc(wq_lo_done, 2)
            pe.wait_ge(const_loaded, CONSTS)

            def turn_raw(i):
                kind, s = items[i][0], i % RAW
                if kind == "B":
                    pe.wait_ge(b_loaded, 16 * E)
                else:
                    pe.wait_ge(raw_loaded[s], raw_count(i))
                if i >= 2:
                    pe.wait_ge(w_lo_done, i - 1)
                out = turn_ps[i % 2]
                for c in range(KC):
                    if kind == "gate":
                        last = pe.transpose(out[:, c, 0:E], raw[0:E, s, c * P:(c + 1) * P], ident[0:E, 0:E])
                    else:
                        last = pe.transpose(out[:, c, :], raw[:, s, c * P:(c + 1) * P], ident[:])
                last.then_inc(raw_turned, 1)

            def turn_h(t):
                pe.wait_ge(h_ready, t + 1)
                pe.wait_ge(hT_lo_done, t)
                if not isinstance(t, int) or t > 0:
                    pe.wait_ge(lowT_lo_done, t)
                    pe.wait_ge(ffn_added, 3 * t)
                for c in range(KC):
                    last = pe.transpose(hT_ps[:, c, :], h[:, c * P:(c + 1) * P], ident[:])
                last.then_inc(h_turned, 1)

            def base(t, par, part):
                cols = slice(PARTS[part].start, WIDE if part == 2 else PARTS[part].stop)
                out = ps[:, 2 + part + (par if part == 2 else 0), 0:cols.stop - cols.start]
                if part < 2:
                    pe.wait_ge(ffn_added, 3 * t + part + 1)
                else:
                    pe.wait_ge(hT_lo_done, t + 1)
                    if not isinstance(t, int) or t > 0:
                        pe.wait_ge(ffn_added, 3 * t)
                for c in range(KC):
                    last = split_products(pe, out, hT_hi[:, par, c, :], hT_lo[:, par, c, :],
                                          wt_hi[:, c, cols], wt_lo[:, c, cols], c == 0, part == 2 and c == KC - 1)
                if part == 2:
                    last.then_inc(gl_done, 1)

            def turn_low(t, more):
                pe.wait_ge(low_ready, t + 1)
                if more:
                    pe.wait_ge(hT_lo_done, t + 2)
                pe.transpose(lowT_ps, low_s[:], ident[:]).then_inc(low_turned, 1)

            def lora(t, par):
                pe.wait_ge(lowT_lo_done, t + 2)
                for part, cols in enumerate(PARTS):
                    out = part_ps(part, par) if part < 2 else last_lora_ps
                    split_products(pe, out, lowT_hi[:], lowT_lo[:], bt_hi[:, cols], bt_lo[:, cols],
                                   part == 2, True).then_inc(ffn_done, 1)

            def project(t, u):
                par = u % 2
                pe.wait_ge(ctx_loaded[par], 32 * (t // 2) + 32)
                for half in range(2):
                    pe.wait_ge(wo_added, 2 * t + half + 1)
                    cols = slice(half * HALF, (half + 1) * HALF)
                    for c in range(KC):
                        last = split_products(pe, wo_ps[:, half, :], ctxT[:, par, 0, c, :], ctxT[:, par, 1, c, :],
                                              wo_hi[:, c, cols], wo_lo[:, c, cols], c == 0, c == KC - 1)
                    last.then_inc(wo_done, 1)

            if attn:
                for t, banks in enumerate((wo_ps, first_ps)):
                    pe.wait_ge(ctx_loaded[t], 32)
                    for c in range(KC):
                        pe.wait_ge(w_lo_done, c + 1)
                        for half in range(2):
                            cols = slice(half * HALF, (half + 1) * HALF)
                            last = split_products(pe, banks[:, half, :], ctxT[:, t, 0, c, :], ctxT[:, t, 1, c, :],
                                                  wo_hi[:, c, cols], wo_lo[:, c, cols], c == 0, c == KC - 1)
                            if c == KC - 1:
                                last.then_inc(wo_done, 1)
            for i in range(min(TURN_H, len(items))):
                turn_raw(i)
            turn_h(0)
            for i in range(TURN_H, len(items) - 1):
                turn_raw(i)
            if prep:
                pe.wait_ge(w_lo_done, len(items) - 1)
            base(0, 0, 2)
            if prep:
                turn_raw(len(items) - 1)
                pe.wait_ge(w_lo_done, len(items))
            if attn:
                pe.wait_ge(wo_added, 2 + 4)

            def step(i, t, u, more):
                if more >= 1:
                    turn_h(t + 1)
                base(t, u % 2, 0)
                turn_low(t, more >= 1)
                if attn and more >= 2:
                    project(t + 2, u + 2)
                base(t, u % 2, 1)
                lora(t, u % 2)
                if more >= 1:
                    base(t + 1, (u + 1) % 2, 2)
            run_tiles(pe, step)

        @block.scalar
        def _(act):
            def high_weight(i):
                kind, k = items[i]
                act.wait_ge(raw_turned, i + 1)
                act.activation(weight_view(kind, k, 0), turned_view(i, kind), ACT.Copy,
                               scale=0.5 if kind == "base" else 1.0).then_inc(w_hi_done, 1)

            def high_hT(t, par):
                act.wait_ge(h_turned, t + 1)
                act.activation(hT_hi[:, par, :, :], hT_ps, ACT.Copy).then_inc(hT_hi_done, 1)

            def deviation(t):
                act.wait_ge(ln_step, 4 * t + 3)
                act.activation(std[:], mv[:, 1:2], ACT.Sqrt, bias=eps[:, 0:1]).then_inc(std_ready, 1)

            act.wait_ge(eps_set, 1)
            if attn:
                for k in range(KC):
                    act.wait_ge(wo_loaded[k % len(wo_raw)], 16 * (k // len(wo_raw) + 1))
                    act.activation(wo_hi[:, k, :], wo_raw[k % len(wo_raw)], ACT.Copy).then_inc(w_hi_done, 1)
            for i in range(min(EARLY, len(items))):
                high_weight(i)
            deviation(0)
            for i in range(EARLY, min(TURN_H, len(items))):
                high_weight(i)
            high_hT(0, 0)
            for i in range(TURN_H, min(NEXT, len(items))):
                high_weight(i)
            deviation(1)
            for i in range(NEXT, len(items)):
                high_weight(i)

            def step(i, t, u, more):
                act.wait_ge(route, ROUTE * t + 3)
                act.activation(expgap[:], gap[:], ACT.Exp).then_inc(exp_done, 1)
                act.wait_ge(ffn_done, 3 * t + 1)
                if more >= 1:
                    high_hT(t + 1, (u + 1) % 2)
                act.wait_ge(low_turned, t + 2)
                act.activation(lowT_hi[:], lowT_ps, ACT.Copy).then_inc(lowT_hi_done, 1)
                if more >= 2:
                    deviation(t + 2)
                if prep:
                    act.wait_ge(wq_loaded[u % 2], (2 * i + u // 2) * 16 + 16)
                    act.activation(wq_piece(0, i, u), wq_raw[:, u % 2, :], ACT.Copy).then_inc(wq_hi_done, 1)
            run_tiles(act, step)

        @block.vector
        def _(dve):
            def low_weight(i):
                kind, k = items[i]
                src = turned_view(i, kind)
                dve.wait_ge(w_hi_done, i + 1)
                if kind == "base":
                    for c in range(0, KC, 4):
                        last = dve.scalar_tensor_tensor(weight_view(kind, k, 1)[:, c:c + 4, :], src[:, c:c + 4, :], 0.5,
                                                 weight_view(kind, k, 0)[:, c:c + 4, :].bitcast(F32), ALU.mult, ALU.subtract)
                    last.then_inc(w_lo_done, 1)
                else:
                    dve.tensor_tensor(weight_view(kind, k, 1), src, weight_view(kind, k, 0).bitcast(F32),
                                      ALU.subtract).then_inc(w_lo_done, 1)

            def layer_norm(i, t, u):
                x = x_ring[:, u % 4, :]
                if attn is None:
                    x_wait(dve, i, u)
                else:
                    dve.wait_ge(wo_added, 2 * t + 4)
                for half in range(2):
                    dve.bn_stats(stats[:, half, :], x[:, half * HALF:(half + 1) * HALF]).then_inc(ln_step, 1)
                wait_apart(dve, ln_step, 4 * t + 2, passed)
                dve.bn_aggr(mv[:], stats[:, :, :].rearrange("p a b -> p (a b)")).then_inc(ln_step, 1)
                dve.wait_ge(std_ready, t + 1)
                dve.reciprocal(rstd[:], std[:]).then_inc(ln_step, 1)
                dve.wait_ge(ln_step, 4 * t + 4)
                dve.wait_ge(h_turned, t)
                dve.tensor_scalar(h[:], x, mv[:, 0:1], rstd[:, 0:1], ALU.subtract, ALU.mult).then_inc(h_ready, 1)

            def low_hT(t, par):
                dve.wait_ge(hT_hi_done, t + 1)
                dve.tensor_tensor(hT_lo[:, par, :, :], hT_ps, hT_hi[:, par, :, :].bitcast(F32),
                                  ALU.subtract).then_inc(hT_lo_done, 1)

            def routing(t, par):
                logits = gl_ps(par, ER, ER + E)
                wait_apart(dve, gl_done, t + 1, passed)
                dve.max(top[:], logits).then_inc(route, 1)
                wait_apart(dve, route, ROUTE * t + 1, passed)
                dve.max_index(top_idx[:], top[:], logits).then_inc(route, 1)
                dve.tensor_tensor(gap[:], top[:, 1:2], top[:, 0:1], ALU.subtract).then_inc(route, 1)
                dve.wait_ge(route, ROUTE * t + 3)
                dve.tensor_copy(idx_f[:], top_idx[:, 0:2]).then_inc(route, 1)
                dve.wait_ge(exp_done, t + 1)
                dve.tensor_scalar(onep[:], expgap[:], 1.0, None, ALU.add).then_inc(route, 1)
                dve.wait_ge(route, ROUTE * t + 5)
                dve.reciprocal(w1[:], onep[:]).then_inc(route, 1)
                dve.wait_ge(route, ROUTE * t + 6)
                dve.tensor_tensor(w2[:], expgap[:], w1[:], ALU.mult).then_inc(route, 1)
                dve.tensor_scalar(wf1[:], expert[:], idx_f[:, 0:1], w1[:, 0:1], ALU.is_equal, ALU.mult).then_inc(route, 1)
                dve.wait_ge(route, ROUTE * t + 8)
                dve.tensor_scalar(wf2[:], expert[:], idx_f[:, 1:2], w2[:, 0:1], ALU.is_equal, ALU.mult).then_inc(route, 1)
                dve.wait_ge(route, ROUTE * t + 9)
                dve.tensor_tensor(w_full[:, :, 0], wf1[:], wf2[:], ALU.add).then_inc(route, 1)
                dve.wait_ge(route, ROUTE * t + 10)
                dve.wait_ge(low_turned, t + 1)
                dve.tensor_tensor(low_s[:].rearrange("p (e r) -> p e r", r=R),
                                  gl_ps(par, 0, ER).rearrange("p (e r) -> p e r", r=R),
                                  w_full[:].broadcast_to([P, E, R]), ALU.mult).then_inc(low_ready, 1)

            def add_projection(i, t, u, banks=wo_ps):
                x_wait(dve, i, u)
                for half in range(2):
                    cols = slice(half * HALF, (half + 1) * HALF)
                    dve.wait_ge(wo_done, 2 * t + half + 1)
                    dve.tensor_tensor(x_ring[:, u % 4, cols], banks[:, half, :], x_ring[:, u % 4, cols],
                                      ALU.add).then_inc(wo_added, 1)

            dve.wait_ge(const_loaded, CONSTS)
            if attn:
                for k in range(KC):
                    dve.wait_ge(w_hi_done, k + 1)
                    dve.tensor_tensor(wo_lo[:, k, :], wo_raw[k % len(wo_raw)], wo_hi[:, k, :].bitcast(F32),
                                      ALU.subtract).then_inc(w_lo_done, 1)
                dve.wait_ge(w_lo_done, KC)
                add_projection(0, 0, 0)
            for i in range(min(EARLY, len(items))):
                low_weight(i)
            layer_norm(0, 0, 0)
            for i in range(EARLY, min(TURN_H, len(items))):
                low_weight(i)
            if attn:
                add_projection(0, 1, 1, first_ps)
            low_hT(0, 0)
            for i in range(TURN_H, min(NEXT, len(items))):
                low_weight(i)
            layer_norm(0, 1, 1)
            for i in range(NEXT, len(items)):
                low_weight(i)

            def step(i, t, u, more):
                routing(t, u % 2)
                if more >= 1:
                    low_hT(t + 1, (u + 1) % 2)
                dve.wait_ge(lowT_hi_done, t + 1)
                dve.tensor_tensor(lowT_lo[:], lowT_ps, lowT_hi[:].bitcast(F32), ALU.subtract).then_inc(lowT_lo_done, 1)
                if more >= 2:
                    if attn:
                        add_projection(i, t + 2, u + 2)
                    layer_norm(i, t + 2, u + 2)
                dve.wait_ge(bias_added, t + 1)
                dve.wait_ge(gl_done, t + 1)
                dve.tensor_tensor(x_ring[:, u, PARTS[2]], part_ps(2, u % 2), x_ring[:, u, PARTS[2]],
                                  ALU.add).then_inc(last_added, 1)
                for part, cols in enumerate(PARTS):
                    dve.wait_ge(ffn_done, 3 * t + (part + 2))
                    if part == 2:
                        dve.wait_ge(last_added, t + 1)
                    src = part_ps(part, u % 2) if part < 2 else last_lora_ps
                    dve.tensor_tensor(x_ring[:, u, cols], src, x_ring[:, u, cols],
                                      ALU.add).then_inc(ffn_added, 1)
            run_tiles(dve, step)


def qkv_stage(nc, x_src, wq, w, consts, scr):
    NCH = T // HALF
    TC = HALF // P
    KV = NKV * DH
    WRAW = 4
    NO = KC + KV // P
    with ExitStack() as ctx:
        def sb(n, shape, dt):
            return ctx.enter_context(nc.sbuf_tensor(f"qkv_{n}", shape, dt))

        def sem(n):
            return ctx.enter_context(nc.semaphore(f"qkv_{n}"))

        wq_hi, wq_lo = wq
        wkv_hi = sb("wkv_hi", [P, KC, 2 * KV], F32R)
        wkv_lo = sb("wkv_lo", [P, KC, 2 * KV], F32R)
        wkv_raw = sb("wkv_raw", [P, WRAW, 2 * KV], F32)
        hT_hi = sb("hT_hi", [P, NCH, KC, HALF], F32R)
        hT_lo = sb("hT_lo", [P, NCH, KC, HALF], F32R)
        x_ring = sb("x_ring", [P, 2, D], F32)
        h = sb("h", [P, D], F32)
        stats = sb("stats", [P, 2, 6], F32)
        mv = sb("mv", [P, 2], F32)
        std = sb("std", [P, 1], F32)
        rstd = sb("rstd", [P, 1], F32)
        eps = sb("eps", [P, 1], F32)
        cos = sb("cos", [P, T], F32)
        sin = sb("sin", [P, T], F32)
        rot = sb("rot", [P, 2, HALF], F32)
        rope = sb("rope", [P, 2, HALF], F32)
        rope_hi = sb("rope_hi", [P, 2, HALF], F32R)
        rope_lo = sb("rope_lo", [P, 2, HALF], F32R)
        v_out = sb("v_out", [P, 2, KV], F32)
        ident = sb("ident", [P, P], F32)

        ps = ctx.enter_context(nc.psum_tensor("qkv_ps", [P, 8, HALF], F32))
        turned_ps = [ps[:, 2 * i:2 * i + 2, :].rearrange("p a (c n) -> p (a c) n", n=P) for i in range(2)]

        wkv_loaded = [sem(f"wkv_loaded{s}") for s in range(WRAW)]
        x_loaded = [sem(f"x_loaded{s}") for s in range(2)]
        passed = sem("passed")
        const_loaded = sem("const_loaded")
        CONSTS = 3 * 16
        eps_set = sem("eps_set")
        wkv_hi_done = sem("wkv_hi_done")
        wkv_lo_done = sem("wkv_lo_done")
        ln_step = sem("ln_step")
        std_ready = sem("std_ready")
        h_ready = sem("h_ready")
        h_turned = sem("h_turned")
        hT_hi_done = sem("hT_hi_done")
        hT_lo_done = sem("hT_lo_done")
        proj_done = sem("proj_done")
        cos_done = sem("cos_done")
        swapped = sem("swapped")
        sin_done = sem("sin_done")
        rope_done = sem("rope_done")
        hi_done = sem("hi_done")
        lo_done = sem("lo_done")
        out_stored = [sem(f"out_stored{s}") for s in range(2)]
        v_done = sem("v_done")
        v_copied = sem("v_copied")
        v_stored = [sem(f"v_stored{s}") for s in range(2)]

        k_rows = scr["k_hi"].rearrange("n r t -> (n r) t"), scr["k_lo"].rearrange("n r t -> (n r) t")

        block = ctx.enter_context(nc.Block())

        def run_chunks(eng, step):
            with eng.Fori(0, B - 1, 1) as b:
                for ch in range(NCH):
                    step(b, ch, True)
            for ch in range(NCH):
                step(B - 1, ch, ch + 1 < NCH)

        @block.sync
        def _(sp):
            sp.dma_start(ident[:], consts["identity"]).then_inc(const_loaded, 16)

            def load_x(t, slot):
                sp.wait_ge(h_ready, t + 1)
                sp.dma_start(x_ring[:, slot, :], x_src[bass.ds(t * P, P), :]).then_inc(x_loaded[slot], 16)

            for t in range(TC):
                load_x(t, t % 2)
            sp.dma_start(cos[:], consts["rope_cos"]).then_inc(const_loaded, 16)
            sp.dma_start(sin[:], consts["rope_sin"]).then_inc(const_loaded, 16)
            for j in range(KC):
                if j >= WRAW:
                    sp.wait_ge(wkv_lo_done, j - WRAW + 1)
                for cols, src in ((slice(0, KV), w["Wk"]), (slice(KV, 2 * KV), w["Wv"])):
                    sp.dma_start(wkv_raw[:, j % WRAW, cols], src[j * P:(j + 1) * P, :]).then_inc(wkv_loaded[j % WRAW], 16)
            with sp.Fori(TC // 2, NT // 2, 1) as i:
                for slot in range(2):
                    load_x(2 * i + slot, slot)

        @block.tensor
        def _(pe):
            pe.sem_inc(h_ready, 2)
            pe.sem_inc(cos_done, 4)
            pe.sem_inc(rope_done, 2)
            pe.sem_inc(lo_done, 2)
            pe.sem_inc(v_copied, 2)
            for first_free in (hT_lo_done, h_turned, v_done, ln_step):
                pe.sem_inc(first_free, 1)
            for first_free in out_stored + v_stored:
                pe.sem_inc(first_free, 16)
            pe.wait_ge(const_loaded, 16)

            def turn_h(b, t, early=False):
                tile = b * (NCH * TC) + t
                pe.wait_ge(h_ready, tile + 3)
                if not early:
                    pe.wait_ge(hT_lo_done, tile + 1)
                elif t:
                    pe.wait_ge(hT_lo_done, t)
                hT_ps = turned_ps[t % 2 if early else 0]
                for c in range(KC):
                    last = pe.transpose(hT_ps[:, c, :], h[:, c * P:(c + 1) * P], ident[:])
                last.then_inc(h_turned, 1)

            for t in range(TC):
                turn_h(0, t, early=True)

            def step(b, ch, more):
                pe.wait_ge(hT_lo_done, b * (NCH * TC) + ((ch + 1) * TC + 1))
                for o in range(NO):
                    g = ch * NO + o
                    if o == KC:
                        pe.wait_ge(wkv_lo_done, KC)
                    pe.wait_ge(cos_done, b * (NCH * NO) + (g + 1))
                    wh, wl = (wq_hi, wq_lo) if o < KC else (wkv_hi, wkv_lo)
                    cols = slice((o % KC) * P, (o % KC + 1) * P)
                    for c in range(KC):
                        last = split_products(pe, ps[:, 2 + g % 4, :], wh[:, c, cols], wl[:, c, cols],
                                              hT_hi[:, ch, c, :], hT_lo[:, ch, c, :], c == 0, c == KC - 1)
                    last.then_inc(proj_done, 1)
                    if more and o % 2 == 1 and o // 2 < TC:
                        turn_h(b, (ch + 1) * TC + o // 2)
                for s in range(TC):
                    t = ch * TC + s
                    pe.wait_ge(v_copied, b * (NCH * TC) + (t + 1))
                    for c in range(KC):
                        tok = slice(s * P, (s + 1) * P)
                        last = split_products(pe, ps[:, 6 + t % 2, 0:KV], hT_hi[:, ch, c, tok], hT_lo[:, ch, c, tok],
                                              wkv_hi[:, c, KV:2 * KV], wkv_lo[:, c, KV:2 * KV], c == 0, c == KC - 1)
                    last.then_inc(v_done, 1)
            run_chunks(pe, step)

        @block.scalar
        def _(act):
            def deviation(b, t):
                act.wait_ge(ln_step, b * (4 * NCH * TC) + (4 * t + 4))
                act.activation(std[:], mv[:, 1:2], ACT.Sqrt, bias=eps[:, 0:1]).then_inc(std_ready, 1)

            def high_hT(b, t, early=False):
                tile = b * (NCH * TC) + t
                act.wait_ge(h_turned, tile + 2)
                act.activation(hT_hi[:, (t // TC) % NCH, :, (t % TC) * P:(t % TC + 1) * P],
                               turned_ps[t % 2 if early else 0], ACT.Copy).then_inc(hT_hi_done, 1)

            def high_out(b, g):
                act.wait_ge(rope_done, b * (NCH * NO) + (g + 3))
                act.wait_ge(out_stored[g % 2], b * (NCH * NO * 16) + (g // 2) * 32 + 16)
                act.activation(rope_hi[:, g % 2, :], rope[:, g % 2, :], ACT.Copy).then_inc(hi_done, 1)

            def store_out(b, g):
                ch, o = g // NO, g % NO
                cols = slice(ch * HALF, (ch + 1) * HALF)
                act.wait_ge(hi_done, b * (NCH * NO) + (g + 1))
                act.wait_ge(lo_done, b * (NCH * NO) + (g + 3))
                for part, buf in enumerate((rope_hi, rope_lo)):
                    q_group = scr[("q_hi", "q_lo")[part]][bass.ds(b * NKV + o % KC, 1), ch, :, :]
                    rows = q_group.rearrange("n r t -> (n r) t") if o < KC \
                        else k_rows[part][bass.ds(b * KV + (o - KC) * P, P), cols]
                    act.dma_start(rows, buf[:, g % 2, :].bitcast(F32)).then_inc(out_stored[g % 2], 16)

            def store_v(b, t):
                act.wait_ge(v_copied, b * (NCH * TC) + (t + 3))
                dst = scr["v"][bass.ds(b * NKV, NKV), t * P:(t + 1) * P, :].rearrange("n t d -> t n d")
                act.dma_start(dst, v_out[:, t % 2, :].rearrange("p (n d) -> p n d", d=DH)).then_inc(v_stored[t % 2], 16)

            act.wait_ge(eps_set, 1)
            deviation(0, 0)
            for t in range(TC):
                if t + 1 < TC:
                    deviation(0, t + 1)
                high_hT(0, t, early=True)
            for j in range(KC):
                act.wait_ge(wkv_loaded[j % WRAW], 32 * (j // WRAW + 1))
                act.activation(wkv_hi[:, j, :], wkv_raw[:, j % WRAW, :], ACT.Copy).then_inc(wkv_hi_done, 1)

            def step(b, ch, more):
                act.wait_ge(v_done, b * (NCH * TC) + (ch * TC + 1))
                for o in range(NO):
                    g = ch * NO + o
                    if more and o % 2 == 0 and o // 2 < TC:
                        deviation(b, (ch + 1) * TC + o // 2)
                    if o >= 1:
                        high_out(b, g - 1)
                    if o >= 2:
                        store_out(b, g - 2)
                    if more and o % 2 == 1 and o // 2 < TC:
                        high_hT(b, (ch + 1) * TC + o // 2)
                for s in range(TC):
                    t = ch * TC + s
                    act.wait_ge(v_done, b * (NCH * TC) + (t + 2))
                    act.wait_ge(v_stored[t % 2], b * (NCH * TC * 8) + (t // 2) * 16 + 16)
                    act.activation(v_out[:, t % 2, :], ps[:, 6 + t % 2, 0:KV], ACT.Copy).then_inc(v_copied, 1)
                    if s == 0:
                        high_out(b, ch * NO + NO - 1)
                    elif s < 3:
                        store_out(b, ch * NO + NO - 3 + s)
                    store_v(b, t)
            run_chunks(act, step)
            for s in range(2):
                act.wait_ge(out_stored[s], B * NCH * NO * 16 + 16)
                act.wait_ge(v_stored[s], B * NCH * TC * 8 + 16)

        @block.gpsimd
        def _(pool):
            pool.memset(eps[:], EPS).then_inc(eps_set, 1)
            for j in range(KC):
                pool.wait_ge(wkv_hi_done, j + 1)
                pool.tensor_tensor(wkv_lo[:, j, :], wkv_raw[:, j % WRAW, :], wkv_hi[:, j, :].bitcast(F32),
                                   ALU.subtract).then_inc(wkv_lo_done, 1)
            pool.wait_ge(const_loaded, CONSTS)

            def low_part(b, g):
                pool.wait_ge(hi_done, b * (NCH * NO) + (g + 1))
                pool.tensor_tensor(rope_lo[:, g % 2, :], rope[:, g % 2, :], rope_hi[:, g % 2, :].bitcast(F32),
                                   ALU.subtract).then_inc(lo_done, 1)

            with pool.Fori(0, B, 1) as b:
                for g in range(NCH * NO):
                    cols = slice((g // NO) * HALF, (g // NO + 1) * HALF)
                    pool.wait_ge(swapped, b * (NCH * NO) + (g + 1))
                    pool.tensor_tensor(rot[:, g % 2, :], rot[:, g % 2, :], sin[:, cols], ALU.mult).then_inc(sin_done, 1)
                    if g % NO >= 1:
                        low_part(b, g - 1)
                    if g % NO == NO - 1:
                        low_part(b, g)

        @block.vector
        def _(dve):
            def moments(b, t):
                dve.wait_ge(x_loaded[t % 2], b * (NCH * TC * 8) + 16 * (t // 2 + 1))
                dve.wait_ge(ln_step, 4 * (b * (NCH * TC) + t) + 1)
                for half in range(2):
                    dve.bn_stats(stats[:, half, :], x_ring[:, t % 2, half * HALF:(half + 1) * HALF]).then_inc(ln_step, 1)
                dve.wait_ge(h_ready, b * (NCH * TC) + (t + 2))
                wait_apart(dve, ln_step, 4 * (b * (NCH * TC) + t) + 3, passed)
                dve.bn_aggr(mv[:], stats[:, :, :].rearrange("p a b -> p (a b)")).then_inc(ln_step, 1)

            def normalize(b, t):
                tile = b * (NCH * TC) + t
                dve.wait_ge(std_ready, tile + 1)
                dve.reciprocal(rstd[:], std[:]).then_inc(ln_step, 1)
                dve.wait_ge(ln_step, 4 * tile + 5)
                dve.wait_ge(h_turned, tile + 1)
                dve.tensor_scalar(h[:], x_ring[:, t % 2, :], mv[:, 0:1], rstd[:, 0:1], ALU.subtract, ALU.mult).then_inc(h_ready, 1)

            def low_hT(b, t, early=False):
                hT_ps = turned_ps[t % 2 if early else 0]
                at = (slice(None), (t // TC) % NCH, slice(None), slice((t % TC) * P, (t % TC + 1) * P))
                dve.wait_ge(hT_hi_done, b * (NCH * TC) + (t + 1))
                dve.tensor_tensor(hT_lo[at], hT_ps, hT_hi[at].bitcast(F32), ALU.subtract).then_inc(hT_lo_done, 1)

            def rope_sum(b, g):
                dve.wait_ge(sin_done, b * (NCH * NO) + (g + 1))
                dve.wait_ge(cos_done, b * (NCH * NO) + (g + 5))
                dve.tensor_tensor(rope[:, g % 2, :], rope[:, g % 2, :], rot[:, g % 2, :], ALU.add).then_inc(rope_done, 1)

            swap = [(i + DH // 2) % DH for i in range(DH)]
            for t in range(TC):
                moments(0, t)
                normalize(0, t)
                if t:
                    low_hT(0, t - 1, early=True)
            low_hT(0, TC - 1, early=True)
            dve.wait_ge(const_loaded, CONSTS)

            def step(b, ch, more):
                cols = slice(ch * HALF, (ch + 1) * HALF)
                for o in range(NO):
                    g = ch * NO + o
                    bank = ps[:, 2 + g % 4, :]
                    if more and o % 2 == 0 and o // 2 < TC:
                        moments(b, (ch + 1) * TC + o // 2)
                        normalize(b, (ch + 1) * TC + o // 2)
                    dve.wait_ge(proj_done, b * (NCH * NO) + (g + 1))
                    wait_apart(dve, rope_done, b * (NCH * NO) + (g + 1), passed)
                    dve.stream_shuffle(rot[:, g % 2, :], bank, swap).then_inc(swapped, 1)
                    dve.wait_ge(lo_done, b * (NCH * NO) + (g + 1))
                    dve.tensor_tensor(rope[:, g % 2, :], bank, cos[:, cols], ALU.mult).then_inc(cos_done, 1)
                    if o >= 1:
                        rope_sum(b, g - 1)
                    if more and o % 2 == 1 and o // 2 < TC:
                        low_hT(b, (ch + 1) * TC + o // 2)
                rope_sum(b, ch * NO + NO - 1)
            run_chunks(dve, step)


def attention_stage(nc, consts, scr, fw, copy):
    NQ = T // P
    QH = NQ // 2
    RING = 3
    SLOTS = 3
    BANKS = 3
    LATE = 1
    LONG = 384
    PROBS = 4
    AHEAD = 2
    KROWS = 3 * DH
    LOADS = 7 * 16
    PIECE = KC * WIDE // NG
    ROW_LOADS = 2 * 16
    SCALE = float(DH) ** -0.5
    with ExitStack() as ctx:
        def sb(n, shape, dt):
            return ctx.enter_context(nc.sbuf_tensor(f"at_{n}", shape, dt))

        def sem(n):
            return ctx.enter_context(nc.semaphore(f"at_{n}"))

        qs = sb("qs", [KROWS + 2, RING, 2, G, HALF], F32R)
        ks = sb("ks", [KROWS + 2, RING, T], F32R)
        vs = sb("vs", [P, RING, NQ, DH], F32)
        ones = sb("ones", [P, DH], F32)
        probs = sb("probs", [P, PROBS, G, HALF], F32)
        row_max = sb("row_max", [P, 2, G, QH], F32)
        part_max = sb("part_max", [P, G, QH], F32)
        neg_hi = sb("neg_hi", [G * QH, 2, P], F32R)
        neg_lo = sb("neg_lo", [G * QH, 2, P], F32R)
        score_mask = sb("score_mask", [P, T], F32)
        ident = sb("ident", [P, P], F32)
        sums = sb("sums", [P, HALF], F32)
        sumT = sb("sumT", [P, HALF // DH, DH], F32)
        recipT = sb("recipT", [P, HALF // DH, 1], F32)
        recip = sb("recip", [P, HALF], F32)
        ctxn = sb("ctxn", [P, 2, HALF], F32)
        ctx_hi = sb("ctx_hi", [P, 2, HALF], F32R)
        ctx_lo = sb("ctx_lo", [P, 2, HALF], F32R)

        ps = ctx.enter_context(nc.psum_tensor("at_ps", [P, 8, HALF], F32))
        slot_ps = [ps[:, b, :] for b in range(SLOTS)]
        score_ps = [ps[:, SLOTS + b, :] for b in range(BANKS)]
        ctx_ps = ps[:, 6, :]
        sum_ps = ps[:, 7, :]

        stacks_loaded = [sem(f"stacks_loaded{r}") for r in range(RING)]
        passed = sem("passed")
        const_loaded = sem("const_loaded")
        const_ready = sem("const_ready")
        early_loaded = sem("early_loaded")
        fw_loaded = sem("fw_loaded")
        slot_filled = sem("slot_filled")
        slot_read = sem("slot_read")
        neg_hi_done = sem("neg_hi_done")
        rows_loaded = [sem(f"rows_loaded{h}") for h in range(2)]
        scores_done = sem("scores_done")
        exp_done = sem("exp_done")
        mask_done = sem("mask_done")
        unit_done = sem("unit_done")
        sum_copied = sem("sum_copied")
        sum_turned = sem("sum_turned")
        recipT_done = sem("recipT_done")
        ctx_copied = sem("ctx_copied")
        recip_done = sem("recip_done")
        mult_done = sem("mult_done")
        chi_done = sem("chi_done")
        clo_done = sem("clo_done")
        ctx_stored = [sem(f"ctx_stored{h}") for h in range(2)]

        units = [(half, j) for half in range(2) for j in range(QH * (half + 1))]
        NU = len(units)
        LAST = {QH - 1: 0, NU - 1: 1}

        def queries(u):
            half, j = units[u]
            return max(half * HALF, j * P), (half + 1) * HALF

        diagonal = [u for u in range(NU) if queries(u)[0] == units[u][1] * P]

        rows = [("row", i, g, c) for i in range(NQ) for c in range(i // QH + 1) for g in range(G)]
        at_a = QH * G + G
        first = rows[:at_a] + [("turn", 0)] + rows[at_a:]
        TURN_B = ("turn", 1)

        def row_keys(i, c):
            return min(HALF, (i + 1) * P - c * HALF)

        weight = [row_keys(it[1], it[3]) + 800 if it[0] == "row" else 900 for it in first]
        room = [queries(u)[1] - queries(u)[0] + 1200 for u in range(NU)]
        places = [[] for _ in range(NU)]
        done, at = 0.0, 0
        for it, wgt in zip(first, weight):
            while at < NU - 1 and sum(room[:at + 1]) / sum(room) < (done + wgt / 2) / sum(weight):
                at += 1
            places[at].append(it)
            done += wgt
        assert len(places[0]) >= SLOTS
        places[0].insert(SLOTS - 1, TURN_B)
        SEQ = len(first) + 1
        PRE = len(first)

        def place_items(u, more):
            if not more:
                return [(0, TURN_B)] if u == 0 else []
            start = sum(len(pl) for pl in places[:u])
            return [(start + x, it) for x, it in enumerate(places[u])]

        def portions(u, items):
            late = LATE if queries(u)[1] - queries(u)[0] >= LONG else 0
            n = max(len(items) - late, 0)
            return [items[n * g // G:n * (g + 1) // G] for g in range(G)] + [items[n:]]

        def position(item, more):
            return next(p for u in range(NU) for p, it in place_items(u, more) if it == item)

        def ahead(n, nm, u, more):
            if u + AHEAD < NU:
                return n, nm, u + AHEAD
            return (n + 1, (nm + 1) % RING, u + AHEAD - NU) if more else None

        q_src = [scr[k].rearrange("n h (g d) t -> n d (h g) t", d=DH) for k in ("q_hi", "q_lo")]

        def first_step_over(n):
            return not isinstance(n, int) or n > 0

        block = ctx.enter_context(nc.Block())

        def steps(eng, step):
            step(0, 0, 0, 2)
            loops = (NG - 2) // RING
            with eng.Fori(0, loops, 1) as i:
                for r in range(RING):
                    step(RING * i + (r + 1), (r + 1) % RING, i + (r + 2) // RING, 2 if NG - 1 - RING * loops >= 2 else 1)
            for n in range(RING * loops + 1, NG):
                step(n, n % RING, (n + 1) // RING, min(NG - 1 - n, 2))

        @block.sync
        def _(sp):
            for dst, k in ((ident[:], "identity"), (score_mask[:, T - P:T], "score_mask")):
                sp.dma_start(dst, consts[k]).then_inc(const_loaded, 16)

            def load_q(n, nm, heads, loaded):
                for row, part in enumerate((0, 0, 1)):
                    dst = qs[row * DH:(row + 1) * DH, nm, :, :, :].rearrange("p h g t -> p (h g) t")
                    sp.dma_start(dst[:, heads, :].bitcast(F32),
                                 q_src[part][bass.ds(n, 1), :, heads, :].rearrange("n d g t -> (n d) g t")).then_inc(loaded, 16)

            def load_k(n, nm, loaded):
                for row, part in enumerate(("k_hi", "k_lo", "k_hi")):
                    sp.dma_start(ks[row * DH:(row + 1) * DH, nm, :].bitcast(F32),
                                 scr[part][bass.ds(n, 1), :, :].rearrange("n d t -> (n d) t")).then_inc(loaded, 16)

            def load_v(n, nm):
                sp.dma_start(vs[:, nm, :, :],
                             scr["v"][bass.ds(n, 1), :, :].rearrange("n (j p) d -> p (n j) d", p=P)).then_inc(stacks_loaded[nm], 16)

            def load(n, nm):
                load_q(n, nm, slice(0, 2 * G), stacks_loaded[nm])
                load_k(n, nm, stacks_loaded[nm])
                load_v(n, nm)

            def load_rows(nm, half, q):
                sp.wait_ge(slot_read, q + (SLOTS + 1))
                for row, src in enumerate((neg_hi, neg_lo)):
                    dst = qs[KROWS + row:KROWS + row + 1, nm, half, :, :].rearrange("p g t -> p (g t)")
                    sp.dma_start(dst.bitcast(F32), src[:, half, :].bitcast(F32)).then_inc(rows_loaded[half], 16)

            def store(n, half):
                sp.wait_ge(clo_done, 2 * n + (half + 3))
                b, kv = n // NKV, n % NKV
                for buf, name in ((ctx_hi, "ctx_hi"), (ctx_lo, "ctx_lo")):
                    dst = scr[name][bass.ds(b * NQ + half * QH, QH), bass.ds(kv, 1), :, :].rearrange("t k p n -> p (t k) n")
                    sp.dma_start(dst, buf[:, half, :].bitcast(F32).rearrange("p (t n) -> p t n", n=P)).then_inc(ctx_stored[half], 16)

            load_k(0, 0, early_loaded)
            load_q(0, 0, slice(0, G), early_loaded)
            load_q(0, 0, slice(G, 2 * G), stacks_loaded[0])
            load_v(0, 0)
            load(1, 1)
            load_rows(0, 0, at_a)
            for part in range(2):
                sp.dma_start(flat(fw["bt"][part]).bitcast(F32), copy["bt"][part]).then_inc(fw_loaded, 16)

            def step(n, nm, _, more):
                load_rows(nm, 1, SEQ * n + (PRE + position(TURN_B, more)))
                if more >= 2:
                    sp.wait_ge(unit_done, NU * n + PROBS)
                    load(n + 2, (nm + 2) % RING)
                for part in range(2):
                    sp.dma_start(flat(fw["wt"][part])[:, bass.ds(n * PIECE, PIECE)].bitcast(F32),
                                 copy["wt"][part][:, bass.ds(n * PIECE, PIECE)]).then_inc(fw_loaded, 16)
                if more:
                    load_rows((nm + 1) % RING, 0, SEQ * n + (PRE + position(("turn", 0), more)))
                if first_step_over(n):
                    store(n - 1, 1)
                store(n, 0)
            steps(sp, step)
            store(NG - 1, 1)
            for half in range(2):
                sp.wait_ge(ctx_stored[half], 32 * NG + 16)
            sp.wait_ge(fw_loaded, 16 * (2 + 2 * NG))

        @block.gpsimd
        def _(pool):
            pool.memset(ones[:], 1.0).then_inc(const_ready, 1)
            pool.memset(score_mask[:, 0:T - P], 0.0).then_inc(const_ready, 1)
            pool.sem_inc(clo_done, 2)

            def mask(n, u):
                tile = probs[:, u % PROBS, :, 0:P]
                wait_apart(pool, exp_done, NU * G * n + (G * (u + 1) + BANKS), passed)
                pool.affine_select(out=tile, in_=tile, compare_op=ALU.is_ge, fill=0.0, base=0,
                                   pattern=[[0, G], [1, P]], channel_multiplier=-1).then_inc(mask_done, 1)

            def divide(n, half):
                pool.wait_ge(recip_done, 2 * n + (half + 2))
                pool.wait_ge(ctx_copied, 2 * n + (half + 2))
                pool.tensor_tensor(ctxn[:, half, :], ctxn[:, half, :], recip[:], ALU.mult).then_inc(mult_done, 1)

            def low(n, half):
                pool.wait_ge(chi_done, 2 * n + (half + 1))
                pool.tensor_tensor(ctx_lo[:, half, :], ctxn[:, half, :], ctx_hi[:, half, :].bitcast(F32),
                                   ALU.subtract).then_inc(clo_done, 1)

            for u in range(AHEAD):
                mask(0, u)

            def step(n, nm, _, more):
                for u in range(NU):
                    a = ahead(n, nm, u, more)
                    if a and a[2] in diagonal:
                        mask(a[0], a[2])
                    if first_step_over(n) and u == 4:
                        divide(n - 1, 1)
                    if first_step_over(n) and u == 6:
                        low(n - 1, 1)
                    if u == 9:
                        divide(n, 0)
                    if u == 11:
                        low(n, 0)
            steps(pool, step)
            divide(NG - 1, 1)
            low(NG - 1, 1)

        @block.tensor
        def _(pe):
            for count, start in ((slot_read, SLOTS), (exp_done, BANKS), (unit_done, PROBS), (sum_copied, 1), (sum_turned, 1), (recipT_done, 1),
                                 (ctx_copied, 1), (recip_done, 1), (mult_done, 1), (rows_loaded[0], 16),
                                 (rows_loaded[1], 16), (ctx_stored[0], 16), (ctx_stored[1], 16)):
                pe.sem_inc(count, start)
            pe.sem_inc(stacks_loaded[0], 3 * 16)
            pe.wait_ge(const_ready, 3)
            pe.wait_ge(const_loaded, 32)

            def slot_item(it, nm, q, slot, all_read=False):
                pe.wait_ge(slot_read, q + (SLOTS if all_read else 1))
                out = slot_ps[slot]
                if it[0] == "turn":
                    pe.transpose(out[0:G * QH, 0:P], row_max[:, it[1], :, :].rearrange("p g q -> p (g q)"),
                                 ident[:]).then_inc(slot_filled, 1)
                    return
                _, i, g, c = it
                keys = row_keys(i, c)
                pe.matmul(out[:, 0:keys], qs[0:KROWS, nm, i // QH, g, (i % QH) * P:(i % QH + 1) * P],
                          ks[0:KROWS, nm, c * HALF:c * HALF + keys], start=True, stop=True).then_inc(slot_filled, 1)

            def scores(n, nm, u, g):
                half, j = units[u]
                a, z = queries(u)
                if j == 0 and g == 0:
                    pe.wait_ge(rows_loaded[half], ROW_LOADS * n + (ROW_LOADS + 16))
                pe.wait_ge(exp_done, NU * G * n + (u * G + g + 1))
                pe.matmul(score_ps[(u * G + g) % BANKS][:, 0:z - a], ks[:, nm, j * P:(j + 1) * P], qs[:, nm, half, g, a - half * HALF:z - half * HALF],
                          start=True, stop=True).then_inc(scores_done, 1)

            def products(n, nm, u, between):
                half, j = units[u]
                a, z = queries(u)
                at = slice(a - half * HALF, z - half * HALF)
                if u in diagonal:
                    pe.wait_ge(mask_done, len(diagonal) * n + (diagonal.index(u) + 1))
                else:
                    pe.wait_ge(exp_done, NU * G * n + (G * (u + 1) + BANKS))
                for bank, stat, copied in ((ctx_ps, vs[:, nm, j, :], ctx_copied), (sum_ps, ones[:], sum_copied)):
                    if j == 0:
                        pe.wait_ge(copied, 2 * n + (half + 1))
                    if bank is sum_ps:
                        between()
                    for g in range(G):
                        last = pe.matmul(bank[g * DH:(g + 1) * DH, at], stat, probs[:, u % PROBS, g, 0:z - a],
                                         start=j == 0, stop=u in LAST)
                last.then_inc(unit_done, 1)

            pe.wait_ge(early_loaded, 6 * 16)
            for q, it in enumerate(first):
                if q == QH * G:
                    pe.wait_ge(stacks_loaded[0], LOADS)
                slot_item(it, 0, q, q % SLOTS)
            for u in range(AHEAD):
                for g in range(G):
                    scores(0, 0, u, g)

            def step(n, nm, turns, more):
                for u in range(NU):
                    portion = portions(u, place_items(u, more))
                    a = ahead(n, nm, u, more)

                    def slot_items(g):
                        for p, it in portion[g]:
                            if it == first[0]:
                                pe.wait_ge(stacks_loaded[(nm + 1) % RING], turns * LOADS + LOADS)
                            slot_item(it, (nm + 1) % RING, SEQ * n + (PRE + p), (PRE + SEQ * nm + p) % SLOTS, not more)

                    for g in range(G):
                        if a:
                            scores(*a, g)
                        slot_items(g)
                    products(n, nm, u, lambda: slot_items(G))
            steps(pe, step)

        @block.scalar
        def _(act):
            def negative(n, half, q, slot):
                act.wait_ge(slot_filled, q + 1)
                act.wait_ge(rows_loaded[half], ROW_LOADS * n + 16)
                act.activation(neg_hi[:, half, :], slot_ps[slot][0:G * QH, 0:P], ACT.Copy, scale=-1.0).then_inc(neg_hi_done, 1)

            def exps(n, u, g):
                a, z = queries(u)
                if g == 0:
                    act.wait_ge(unit_done, NU * n + (u + 1))
                act.wait_ge(scores_done, NU * G * n + (u * G + g + 1))
                act.activation(probs[:, u % PROBS, g, 0:z - a], score_ps[(u * G + g) % BANKS][:, 0:z - a], ACT.Exp,
                               scale=SCALE).then_inc(exp_done, 1)

            def copy_chunk(n, half):
                act.wait_ge(unit_done, NU * n + (PROBS + (QH, NU)[half]))
                act.wait_ge(clo_done, 2 * n + (half + 1))
                act.activation(ctxn[:, half, :], ctx_ps, ACT.Copy).then_inc(ctx_copied, 1)
                act.wait_ge(sum_turned, 2 * n + (half + 1))
                act.activation(sums[:], sum_ps, ACT.Copy).then_inc(sum_copied, 1)

            def high(n, half):
                act.wait_ge(mult_done, 2 * n + (half + 2))
                act.wait_ge(ctx_stored[half], 32 * n + 16)
                act.activation(ctx_hi[:, half, :], ctxn[:, half, :], ACT.Copy).then_inc(chi_done, 1)

            negative(0, 0, at_a, at_a % SLOTS)
            for u in range(AHEAD):
                for g in range(G):
                    exps(0, u, g)

            def step(n, nm, _, more):
                for u in range(NU):
                    portion = portions(u, place_items(u, more))
                    a = ahead(n, nm, u, more)
                    for g in range(G + 1):
                        if a and g < G:
                            exps(a[0], a[2], g)
                        for p, it in portion[g]:
                            if it[0] == "turn":
                                negative(n if it[1] else n + 1, it[1], SEQ * n + (PRE + p), (PRE + SEQ * nm + p) % SLOTS)
                    if u in LAST:
                        copy_chunk(n, LAST[u])
                    if first_step_over(n) and u == 5:
                        high(n - 1, 1)
                    if u == 10:
                        high(n, 0)
            steps(act, step)
            high(NG - 1, 1)

        @block.vector
        def _(dve):
            dve.memset(ks[KROWS:KROWS + 2, :, :].bitcast(F32), 1.0).then_inc(const_ready, 1)
            dve.wait_ge(const_loaded, 32)
            dve.wait_ge(const_ready, 3)

            def slot_item(it, n, q, slot):
                if it[0] == "turn":
                    dve.wait_ge(neg_hi_done, 2 * n + (it[1] + 1))
                    dve.scalar_tensor_tensor(neg_lo[:, it[1], :], slot_ps[slot][0:G * QH, 0:P], -1.0,
                                             neg_hi[:, it[1], :].bitcast(F32), ALU.mult, ALU.subtract).then_inc(slot_read, 1)
                    return
                _, i, g, c = it
                keys = row_keys(i, c)
                src = slot_ps[slot][:, 0:keys]
                half, tile = i // QH, i % QH
                own = slice(tile, tile + 1)
                whole = c == half
                mask = score_mask[:, T - keys:T] if whole else score_mask[:, 0:keys]
                out = row_max[:, half, g, own] if whole else part_max[:, g, own]
                if c:
                    dve.wait_ge(slot_read, q + (SLOTS - G + 1))
                wait_apart(dve, slot_filled, q + 1, passed)
                dve.tensor_tensor_reduce(out=src, in0=src, in1=mask, scale=1.0, scalar=part_max[:, g, own] if c else -3.0e38,
                                         op0=ALU.add, op1=ALU.max, accum_out=out).then_inc(slot_read, 1)

            def reciprocal(n, half):
                chunk = 2 * n + (half + 1)
                dve.wait_ge(recipT_done, chunk)
                wait_apart(dve, sum_copied, chunk + 1, passed)
                dve.transpose(sumT[:].rearrange("p c n -> p (c n)"), sums[:]).then_inc(sum_turned, 1)
                dve.wait_ge(recip_done, chunk)
                dve.wait_ge(sum_turned, chunk + 1)
                dve.reciprocal(recipT[:], sumT[:, :, 0:1]).then_inc(recipT_done, 1)
                dve.wait_ge(mult_done, chunk)
                wait_apart(dve, recipT_done, chunk + 1, passed)
                dve.transpose(recip[:], recipT[:].broadcast_to([P, HALF // DH, DH])).then_inc(recip_done, 1)

            for q, it in enumerate(first):
                slot_item(it, 0, q, q % SLOTS)

            def step(n, nm, _, more):
                for u in range(NU):
                    for p, it in place_items(u, more):
                        slot_item(it, n if it == TURN_B else n + 1, SEQ * n + (PRE + p), (PRE + SEQ * nm + p) % SLOTS)
                    if first_step_over(n) and u == 1:
                        reciprocal(n - 1, 1)
                    if u == 5:
                        reciprocal(n, 0)
            steps(dve, step)
            reciprocal(NG - 1, 1)


def build(nc, ins, consts, out):
    x = ins["L0_attn_resid"].rearrange("b t d -> (b t) d")
    y = out.rearrange("b t d -> (b t) d")
    raw = {k: ins["L0_ffn_" + k] for k in ("gate_w", "base_w", "lora_A", "lora_B")}
    base_b = ins["L0_ffn_base_b"]
    attn_w = {k: ins["L0_attn_" + k] for k in ("Wk", "Wv")}
    x1 = nc.dram_tensor("x1", (N, D), F32).ap()
    scr = {k: nc.dram_tensor(f"scr_{k}", shape, dt).ap() for k, shape, dt in (
        ("q_hi", (NG, T // HALF, G * DH, HALF), F32), ("q_lo", (NG, T // HALF, G * DH, HALF), F32),
        ("k_hi", (NG, DH, T), F32), ("k_lo", (NG, DH, T), F32), ("v", (NG, T, DH), F32),
        ("ctx_hi", (NT, NKV, P, P), F32), ("ctx_lo", (NT, NKV, P, P), F32))}
    copy = {k: [nc.dram_tensor(f"copy_{k}_{part}", (P, n), F32).ap() for part in ("hi", "lo")]
            for k, n in (("wt", KC * WIDE), ("bt", D))}
    with ExitStack() as ctx:
        wq = [ctx.enter_context(nc.sbuf_tensor(f"wq_{part}", [P, KC, D], F32R)) for part in ("hi", "lo")]
        with ExitStack() as inner:
            fw = ffn_weights(nc, inner, "f1")
            ffn_stage(nc, "f1", x, x1, fw, base_b, consts, prep={"wq": wq, "Wq": ins["L0_attn_Wq"], "copy": copy, **raw})
        qkv_stage(nc, x1, wq, attn_w, consts, scr)
    with ExitStack() as ctx:
        fw = ffn_weights(nc, ctx, "f2")
        attention_stage(nc, consts, scr, fw, copy)
        ffn_stage(nc, "f2", x1, y, fw, base_b, consts,
                  attn={"wo": ins["L0_attn_Wo"], "ctx_hi": scr["ctx_hi"], "ctx_lo": scr["ctx_lo"]})


def shape_constants():
    f = np.float32
    idx = np.arange(0, DH, 2, dtype=f) / f(DH)
    freq = f(1.0 / (2.0 * np.pi)) * np.power(f(500000.0), -idx)
    factor, lo, hi, length = 32.0, 1.0, 4.0, 2048
    scaled = np.where(freq < f(lo / length), freq / f(factor), freq)
    smooth = np.clip((f(length) * freq - f(lo)) / f(hi - lo), f(0), f(1))
    mid = (freq >= f(lo / length)) & (freq <= f(hi / length))
    freq = np.where(mid, (f(1) - smooth) * (freq / f(factor)) + smooth * freq, scaled).astype(f)
    phase = f(2.0 * np.pi) * np.arange(T, dtype=f)[None, :] * freq[:, None]
    sign = np.concatenate([-np.ones(DH // 2, f), np.ones(DH // 2, f)])[:, None]
    cos = np.tile(np.cos(phase), (2, 1)).astype(f)
    sin = (np.tile(np.sin(phase), (2, 1)) * sign).astype(f)
    above = np.triu(np.full((P, P), NEG, f), 1)
    return {"identity": np.eye(P, dtype=f), "expert": np.tile(np.arange(E, dtype=f), (P, 1)),
            "rope_cos": np.tile(cos, (P // DH, 1)), "rope_sin": np.tile(sin, (P // DH, 1)),
            "score_mask": above}


def kernel(**inputs):
    import concourse.bacc as bacc
    from concourse.bass_utils import run_bass_kernel_spmd

    nc = bacc.Bacc("TRN2", target_bir_lowering=False, num_devices=1)
    arrays, ins, consts = {}, {}, {}
    for group, named in ((ins, inputs), (consts, shape_constants())):
        for k, a in named.items():
            a = np.ascontiguousarray(a)
            arrays["in_" + k] = a
            group[k] = nc.dram_tensor("in_" + k, a.shape, mybir.dt.from_np(a.dtype), kind="ExternalInput").ap()
    out = nc.dram_tensor("out_x", (B, T, D), F32, kind="ExternalOutput").ap()
    build(nc, ins, consts, out)
    r = run_bass_kernel_spmd(nc, [arrays], core_ids=[0])
    return r.results[0]["out_x"]
```
